# Optimizing a Trainium2 kernel written in Bass

```python
import numpy as np
import jax
import jax.numpy as jnp

def _softmax(x, axis=-1):
    return jax.nn.softmax(x, axis=axis)

def _gelu(x):
    return jax.nn.gelu(x, approximate=True)

def _silu(x):
    return jax.nn.silu(x)

def _sigmoid(x):
    return jax.nn.sigmoid(x)

def _layernorm(x, axis=-1, eps=1e-05):
    m = jnp.mean(x, axis=axis, keepdims=True)
    v = jnp.var(x, axis=axis, keepdims=True)
    return (x - m) / jnp.sqrt(v + eps)

def _scatter_add(tgt, idx, src, axis=0):
    return tgt.at[idx].add(src)

def _segment_sum(src, seg, n):
    return jax.ops.segment_sum(src, seg, n)
kernel_name = 'mk_gnn_ffn_d4_gnn_r8_4c58d2'

def setup_inputs(seed: int=0):
    np.random.seed(seed)
    _w = jnp.asarray

    def _rec_inputs():
        import jax
        import jax.numpy as jnp
        _gk = jax.random.key(seed)
        x = -0.0003713 + 1 * jax.random.normal(jax.random.fold_in(_gk, 1), (6250, 256), jnp.float32)
        src = jax.random.randint(jax.random.fold_in(_gk, 2), (100000,), 0, 6250, jnp.int32)
        dst = jnp.minimum((6250 * jax.random.uniform(jax.random.fold_in(_gk, 3), (100000,)) ** 2.0).astype(jnp.int32), 49999)
        _o = jnp.argsort(dst, stable=True)
        src = src[_o]
        dst = dst[_o]
        edge_attr_64 = 5.96457e-05 + 0.999887 * jax.random.normal(jax.random.fold_in(_gk, 12), (100000, 64), jnp.float32)
        node_vec1 = jax.random.uniform(jax.random.fold_in(_gk, 14), (6250, 1), jnp.float32, 0.0, 0.999943)
        return (x, src, dst, edge_attr_64, node_vec1)
    x, src, dst, edge_attr_64, node_vec1 = _rec_inputs()

    def _L0_gnn_setup():
        import jax, jax.numpy as jnp
        import numpy as np
        N = 6250
        E = 100000
        D = 256
        H = 4
        C = 64
        EPS = 1e-05

        def _layernorm(x, gamma, beta):
            mu = jnp.mean(x, axis=-1, keepdims=True)
            var = jnp.mean(jnp.square(x - mu), axis=-1, keepdims=True)
            return (x - mu) * jax.lax.rsqrt(var + EPS) * gamma + beta
        key = jax.random.key(seed)
        ks = jax.random.split(key, 12)
        s = 1.0 / np.sqrt(D)
        return {'x': jax.random.normal(ks[0], (N, D), dtype=jnp.float32), 'edge_index': jax.random.randint(ks[1], (2, E), 0, N, dtype=jnp.int64), 'ln_gamma': jnp.ones((D,), jnp.float32), 'ln_beta': jnp.zeros((D,), jnp.float32), 'Wq': jax.random.normal(ks[2], (D, H * C), dtype=jnp.float32) * s, 'bq': jnp.zeros((H * C,), jnp.float32), 'Wk': jax.random.normal(ks[3], (D, H * C), dtype=jnp.float32) * s, 'bk': jnp.zeros((H * C,), jnp.float32), 'Wv': jax.random.normal(ks[4], (D, H * C), dtype=jnp.float32) * s, 'bv': jnp.zeros((H * C,), jnp.float32), 'Wskip': jax.random.normal(ks[5], (D, H * C), dtype=jnp.float32) * s, 'bskip': jnp.zeros((H * C,), jnp.float32)}
    _L0_gnn_all = _L0_gnn_setup()
    _L0_gnn_in = {k: v for k, v in _L0_gnn_all.items() if k in ('ln_gamma', 'ln_beta', 'Wq', 'bq', 'Wk', 'bk', 'Wv', 'bv', 'Wskip', 'bskip')}
    del _L0_gnn_all

    def _L0_ffn_setup():
        import jax, jax.numpy as jnp
        import numpy as np
        E = 8
        K = 2
        D = 256
        H = 512
        DOUT = 256
        EPS = 1e-05
        key = jax.random.key(seed)
        ks = jax.random.split(key, 9)
        s = 0.02
        return {'x': jax.random.normal(ks[0], (4, 1024, D), jnp.float32), 'gamma': 1.0 + 0.05 * jax.random.normal(ks[1], (D,), jnp.float32), 'beta': 0.05 * jax.random.normal(ks[2], (D,), jnp.float32), 'Wr': 0.01 * jax.random.normal(ks[3], (D, E), jnp.float32), 'br': jnp.zeros((E,), jnp.float32), 'W1': s * jax.random.normal(ks[4], (E, D, H), jnp.float32), 'b1': s * jax.random.normal(ks[5], (E, H), jnp.float32), 'W2': s * jax.random.normal(ks[6], (E, H, DOUT), jnp.float32), 'b2': s * jax.random.normal(ks[7], (E, DOUT), jnp.float32)}
    _L0_ffn_all = _L0_ffn_setup()
    _L0_ffn_in = {k: v for k, v in _L0_ffn_all.items() if k in ('gamma', 'beta', 'Wr', 'br', 'W1', 'b1', 'W2', 'b2')}
    del _L0_ffn_all

    def _L1_gnn_setup():
        import jax, jax.numpy as jnp
        import numpy as np
        N_NODES = 6250
        N_EDGES = 100000
        D_IN = 256
        D_OUT = 256
        key = jax.random.key(seed)
        k1, k2, k3, k4 = jax.random.split(key, 4)
        bound = 1.0 / np.sqrt(D_IN)
        vertex_features = jax.random.normal(k1, (N_NODES, D_IN), dtype=jnp.float32)
        edge_index = jax.random.randint(k2, (2, N_EDGES), 0, N_NODES, dtype=jnp.int32)
        w0 = jax.random.uniform(k3, (D_IN, D_OUT), minval=-bound, maxval=bound, dtype=jnp.float32)
        w1 = jax.random.uniform(k4, (D_IN, D_OUT), minval=-bound, maxval=bound, dtype=jnp.float32)
        return {'vertex_features': vertex_features, 'edge_index': edge_index, 'w0': w0, 'w1': w1}
    _L1_gnn_all = _L1_gnn_setup()
    _L1_gnn_in = {k: v for k, v in _L1_gnn_all.items() if k in ('w0', 'w1')}
    del _L1_gnn_all

    def _L1_ffn_setup():
        import jax, jax.numpy as jnp
        import numpy as np
        B, N, D = (16, 512, 256)
        NUM_EXPERTS, TOP_K, HEADS = (4, 2, 4)
        N_EDGES = 131072
        LN_EPS = 1e-05

        def _layernorm(x, g, b):
            mu = x.mean(-1, keepdims=True)
            var = ((x - mu) ** 2).mean(-1, keepdims=True)
            return (x - mu) * jax.lax.rsqrt(var + LN_EPS) * g + b

        def _forward(x, edge_index, W_gat, att_src, att_dst, b_gat, ln_gamma, ln_beta, W1, b1, W2, b2):
            Bc, Nc, Dc = x.shape
            M = Bc * Nc
            x_flat = x.reshape(M, Dc)
            h = (x_flat @ W_gat).reshape(M, HEADS, NUM_EXPERTS)
            loops = jnp.arange(M, dtype=edge_index.dtype)
            src = jnp.concatenate([edge_index[0], loops])
            dst = jnp.concatenate([edge_index[1], loops])
            a_src = (h * att_src).sum(-1)
            a_dst = (h * att_dst).sum(-1)
            e = jax.nn.leaky_relu(a_src[src] + a_dst[dst], negative_slope=0.2)
            e_max = jax.ops.segment_max(e, dst, num_segments=M)
            ee = jnp.exp(e - e_max[dst])
            denom = jax.ops.segment_sum(ee, dst, num_segments=M)
            alpha = ee / (denom[dst] + 1e-16)
            msg = h[src] * alpha[:, :, None]
            agg = jax.ops.segment_sum(msg, dst, num_segments=M).reshape(M, HEADS * NUM_EXPERTS) + b_gat
            scores = _layernorm(agg, ln_gamma, ln_beta).reshape(M, HEADS, NUM_EXPERTS).mean(1)
            scores = scores.reshape(Bc, Nc, NUM_EXPERTS)
            topk_s, topk_i = jax.lax.top_k(scores, TOP_K)
            w = jax.nn.softmax(topk_s, axis=-1)
            out = jnp.zeros_like(x)
            for ei in range(NUM_EXPERTS):
                g = jnp.where(topk_i == ei, w, 0.0).sum(-1)
                hh = jax.nn.gelu(x @ W1[ei] + b1[ei], approximate=False)
                out = out + g[..., None] * (hh @ W2[ei] + b2[ei])
            return out
        key = jax.random.key(seed)
        ks = jax.random.split(key, 8)
        s = 0.05
        return {'x': jax.random.normal(ks[0], (B, N, D), jnp.float32), 'W_gat': jax.random.normal(ks[1], (D, HEADS * NUM_EXPERTS), jnp.float32) * s, 'att_src': jax.random.normal(ks[2], (HEADS, NUM_EXPERTS), jnp.float32) * s, 'att_dst': jax.random.normal(ks[3], (HEADS, NUM_EXPERTS), jnp.float32) * s, 'b_gat': jnp.zeros((HEADS * NUM_EXPERTS,), jnp.float32), 'ln_gamma': jnp.ones((HEADS * NUM_EXPERTS,), jnp.float32), 'ln_beta': jnp.zeros((HEADS * NUM_EXPERTS,), jnp.float32), 'W1': jax.random.normal(ks[4], (NUM_EXPERTS, D, 2 * D), jnp.float32) * s, 'b1': jnp.zeros((NUM_EXPERTS, 2 * D), jnp.float32), 'W2': jax.random.normal(ks[5], (NUM_EXPERTS, 2 * D, D), jnp.float32) * s, 'b2': jnp.zeros((NUM_EXPERTS, D), jnp.float32), 'edge_index': jax.random.randint(ks[6], (2, N_EDGES), 0, B * N, jnp.int32)}
    _L1_ffn_all = _L1_ffn_setup()
    _L1_ffn_in = {k: v for k, v in _L1_ffn_all.items() if k in ('W_gat', 'att_src', 'att_dst', 'b_gat', 'ln_gamma', 'ln_beta', 'W1', 'b1', 'W2', 'b2', 'edge_index')}
    del _L1_ffn_all

    def _L2_gnn_setup():
        import jax, jax.numpy as jnp
        import numpy as np
        N_NODES = 1250
        N_EDGES = 20000
        IN_FEATS = 256
        E_DIMS = 64
        NEG_SLOPE = 0.01
        key = jax.random.key(seed)
        ks = jax.random.split(key, 8)
        h = jax.random.normal(ks[0], (N_NODES, IN_FEATS), dtype=jnp.float32)
        w = jax.random.normal(ks[1], (N_EDGES, E_DIMS), dtype=jnp.float32)
        snorm_n = jax.random.uniform(ks[2], (N_NODES, 1), dtype=jnp.float32)
        edge_src = jax.random.randint(ks[3], (N_EDGES,), 0, N_NODES, dtype=jnp.int64)
        edge_dst = jax.random.randint(ks[4], (N_EDGES,), 0, N_NODES, dtype=jnp.int64)
        W_self = jax.random.normal(ks[5], (IN_FEATS, IN_FEATS), dtype=jnp.float32) * np.sqrt(2.0 / IN_FEATS)
        W_func = jax.random.normal(ks[6], (IN_FEATS, IN_FEATS), dtype=jnp.float32) * np.sqrt(2.0 / IN_FEATS)
        W_att = jax.random.normal(ks[7], (1, 2 * IN_FEATS + E_DIMS), dtype=jnp.float32) * np.sqrt(2.0 / (2 * IN_FEATS + E_DIMS))
        return {'h': h, 'w': w, 'snorm_n': snorm_n, 'edge_src': edge_src, 'edge_dst': edge_dst, 'W_self': W_self, 'W_func': W_func, 'W_att': W_att}
    _L2_gnn_all = _L2_gnn_setup()
    _L2_gnn_in = {k: v for k, v in _L2_gnn_all.items() if k in ('W_self', 'W_func', 'W_att')}
    del _L2_gnn_all

    def _L2_ffn_setup():
        import jax, jax.numpy as jnp
        import numpy as np
        NUM_EXPERTS = 8
        TOP_K = 2
        B, S, D = (8, 1024, 256)

        def _moe(tokens, router_w, w1, b1, w2, b2):
            N = tokens.shape[0]
            E = router_w.shape[0]
            logits = tokens.astype(jnp.float32) @ router_w.astype(jnp.float32).T
            probs = jax.nn.softmax(logits, axis=-1)
            rw, re = jax.lax.top_k(probs, TOP_K)
            if TOP_K > 1:
                rw = rw / jnp.maximum(rw.sum(-1, keepdims=True), 1e-12)
            rw = rw.astype(tokens.dtype)
            combine = jnp.zeros((N, E), tokens.dtype).at[jnp.arange(N)[:, None], re].set(rw)
            out = tokens
            for e in range(E):
                h = jax.nn.gelu(tokens @ w1[e] + b1[e], approximate=False)
                y = h @ w2[e] + b2[e]
                out = out + combine[:, e:e + 1] * y
            return out
        key = jax.random.key(seed)
        ks = jax.random.split(key, 4)
        scale = 1.0 / np.sqrt(D).astype(np.float32)
        return {'input_embeddings': jax.random.normal(ks[0], (B, S, D), jnp.float32), 'router_w': jax.random.normal(ks[1], (NUM_EXPERTS, D), jnp.float32) * scale, 'w1': jax.random.normal(ks[2], (NUM_EXPERTS, D, D), jnp.float32) * scale, 'b1': jnp.zeros((NUM_EXPERTS, D), jnp.float32), 'w2': jax.random.normal(ks[3], (NUM_EXPERTS, D, D), jnp.float32) * scale, 'b2': jnp.zeros((NUM_EXPERTS, D), jnp.float32)}
    _L2_ffn_all = _L2_ffn_setup()
    _L2_ffn_in = {k: v for k, v in _L2_ffn_all.items() if k in ('router_w', 'w1', 'b1', 'w2', 'b2')}
    del _L2_ffn_all

    def _L3_gnn_setup():
        import jax, jax.numpy as jnp
        import numpy as np
        N, IN_CH, HEADS, OUT_CH, E = (6250, 256, 4, 64, 100000)
        key = jax.random.key(seed)
        k1, k2, k3, k4, k5 = jax.random.split(key, 5)
        x = jax.random.normal(k1, (N, IN_CH), dtype=jnp.float32)
        edge_index = jax.random.randint(k2, (2, E), 0, N, dtype=jnp.int64)
        bw = float(np.sqrt(6.0 / (IN_CH + HEADS * OUT_CH)))
        ba = float(np.sqrt(6.0 / (HEADS + OUT_CH)))
        weight = jax.random.uniform(k3, (IN_CH, HEADS * OUT_CH), jnp.float32, -bw, bw)
        attn_l = jax.random.uniform(k4, (HEADS, OUT_CH), jnp.float32, -ba, ba)
        attn_r = jax.random.uniform(k5, (HEADS, OUT_CH), jnp.float32, -ba, ba)
        return {'x': x, 'edge_index': edge_index, 'weight': weight, 'attn_l': attn_l, 'attn_r': attn_r}
    _L3_gnn_all = _L3_gnn_setup()
    _L3_gnn_in = {k: v for k, v in _L3_gnn_all.items() if k in ('weight', 'attn_l', 'attn_r')}
    del _L3_gnn_all

    def _L3_ffn_setup():
        import math
        import jax, jax.numpy as jnp
        import numpy as np
        CAPACITY_FACTOR = 1.25
        key = jax.random.key(seed)
        ks = jax.random.split(key, 5)
        B, L, D, F, E = (8, 1024, 256, 1024, 8)
        h = jax.random.normal(ks[0], (B, L, D), dtype=jnp.float32)
        gate_w = jax.random.normal(ks[1], (D, E), dtype=jnp.float32) * 0.02
        gate_b = jnp.zeros((E,), dtype=jnp.float32)
        w1 = jax.random.normal(ks[2], (E, D, F), dtype=jnp.float32) * (1.0 / math.sqrt(D))
        b1 = jnp.zeros((E, F), dtype=jnp.float32)
        w2 = jax.random.normal(ks[3], (E, F, D), dtype=jnp.float32) * (1.0 / math.sqrt(F))
        b2 = jnp.zeros((E, D), dtype=jnp.float32)
        return {'h': h, 'gate_w': gate_w, 'gate_b': gate_b, 'w1': w1, 'b1': b1, 'w2': w2, 'b2': b2}
    _L3_ffn_all = _L3_ffn_setup()
    _L3_ffn_in = {k: v for k, v in _L3_ffn_all.items() if k in ('gate_w', 'gate_b', 'w1', 'b1', 'w2', 'b2')}
    del _L3_ffn_all
    return {'x': x, 'src': src, 'dst': dst, 'edge_attr_64': edge_attr_64, 'node_vec1': node_vec1, 'L0_gnn_ln_gamma': _L0_gnn_in['ln_gamma'], 'L0_gnn_ln_beta': _L0_gnn_in['ln_beta'], 'L0_gnn_Wq': _L0_gnn_in['Wq'], 'L0_gnn_bq': _L0_gnn_in['bq'], 'L0_gnn_Wk': _L0_gnn_in['Wk'], 'L0_gnn_bk': _L0_gnn_in['bk'], 'L0_gnn_Wv': _L0_gnn_in['Wv'], 'L0_gnn_bv': _L0_gnn_in['bv'], 'L0_gnn_Wskip': _L0_gnn_in['Wskip'], 'L0_gnn_bskip': _L0_gnn_in['bskip'], 'L0_ffn_gamma': _L0_ffn_in['gamma'], 'L0_ffn_beta': _L0_ffn_in['beta'], 'L0_ffn_Wr': _L0_ffn_in['Wr'], 'L0_ffn_br': _L0_ffn_in['br'], 'L0_ffn_W1': _L0_ffn_in['W1'], 'L0_ffn_b1': _L0_ffn_in['b1'], 'L0_ffn_W2': _L0_ffn_in['W2'], 'L0_ffn_b2': _L0_ffn_in['b2'], 'L1_gnn_w0': _L1_gnn_in['w0'], 'L1_gnn_w1': _L1_gnn_in['w1'], 'L1_ffn_W_gat': _L1_ffn_in['W_gat'], 'L1_ffn_att_src': _L1_ffn_in['att_src'], 'L1_ffn_att_dst': _L1_ffn_in['att_dst'], 'L1_ffn_b_gat': _L1_ffn_in['b_gat'], 'L1_ffn_ln_gamma': _L1_ffn_in['ln_gamma'], 'L1_ffn_ln_beta': _L1_ffn_in['ln_beta'], 'L1_ffn_W1': _L1_ffn_in['W1'], 'L1_ffn_b1': _L1_ffn_in['b1'], 'L1_ffn_W2': _L1_ffn_in['W2'], 'L1_ffn_b2': _L1_ffn_in['b2'], 'L1_ffn_edge_index': _L1_ffn_in['edge_index'], 'L2_gnn_W_self': _L2_gnn_in['W_self'], 'L2_gnn_W_func': _L2_gnn_in['W_func'], 'L2_gnn_W_att': _L2_gnn_in['W_att'], 'L2_ffn_router_w': _L2_ffn_in['router_w'], 'L2_ffn_w1': _L2_ffn_in['w1'], 'L2_ffn_b1': _L2_ffn_in['b1'], 'L2_ffn_w2': _L2_ffn_in['w2'], 'L2_ffn_b2': _L2_ffn_in['b2'], 'L3_gnn_weight': _L3_gnn_in['weight'], 'L3_gnn_attn_l': _L3_gnn_in['attn_l'], 'L3_gnn_attn_r': _L3_gnn_in['attn_r'], 'L3_ffn_gate_w': _L3_ffn_in['gate_w'], 'L3_ffn_gate_b': _L3_ffn_in['gate_b'], 'L3_ffn_w1': _L3_ffn_in['w1'], 'L3_ffn_b1': _L3_ffn_in['b1'], 'L3_ffn_w2': _L3_ffn_in['w2'], 'L3_ffn_b2': _L3_ffn_in['b2']}

def reference(x, src, dst, edge_attr_64, node_vec1, L0_gnn_ln_gamma, L0_gnn_ln_beta, L0_gnn_Wq, L0_gnn_bq, L0_gnn_Wk, L0_gnn_bk, L0_gnn_Wv, L0_gnn_bv, L0_gnn_Wskip, L0_gnn_bskip, L0_ffn_gamma, L0_ffn_beta, L0_ffn_Wr, L0_ffn_br, L0_ffn_W1, L0_ffn_b1, L0_ffn_W2, L0_ffn_b2, L1_gnn_w0, L1_gnn_w1, L1_ffn_W_gat, L1_ffn_att_src, L1_ffn_att_dst, L1_ffn_b_gat, L1_ffn_ln_gamma, L1_ffn_ln_beta, L1_ffn_W1, L1_ffn_b1, L1_ffn_W2, L1_ffn_b2, L1_ffn_edge_index, L2_gnn_W_self, L2_gnn_W_func, L2_gnn_W_att, L2_ffn_router_w, L2_ffn_w1, L2_ffn_b1, L2_ffn_w2, L2_ffn_b2, L3_gnn_weight, L3_gnn_attn_l, L3_gnn_attn_r, L3_ffn_gate_w, L3_ffn_gate_b, L3_ffn_w1, L3_ffn_b1, L3_ffn_w2, L3_ffn_b2):
    import jax
    import jax.numpy as jnp

    def _L0_gnn_ref(x, edge_index, ln_gamma, ln_beta, Wq, bq, Wk, bk, Wv, bv, Wskip, bskip):
        import jax, jax.numpy as jnp
        import numpy as np
        N = 6250
        E = 100000
        D = 256
        H = 4
        C = 64
        EPS = 1e-05

        def _layernorm(x, gamma, beta):
            mu = jnp.mean(x, axis=-1, keepdims=True)
            var = jnp.mean(jnp.square(x - mu), axis=-1, keepdims=True)
            return (x - mu) * jax.lax.rsqrt(var + EPS) * gamma + beta
        h = _layernorm(x, ln_gamma, ln_beta)
        q = (h @ Wq + bq).reshape(N, H, C)
        k = (h @ Wk + bk).reshape(N, H, C)
        v = (h @ Wv + bv).reshape(N, H, C)
        src, dst = (edge_index[0], edge_index[1])
        score = jnp.einsum('ehc,ehc->eh', q[dst], k[src]) / np.sqrt(C)
        m = jax.ops.segment_max(score, dst, num_segments=N)
        ex = jnp.exp(score - m[dst])
        denom = jax.ops.segment_sum(ex, dst, num_segments=N)
        alpha = ex / denom[dst]
        msg = alpha[:, :, None] * v[src]
        agg = jax.ops.segment_sum(msg, dst, num_segments=N)
        out = agg.reshape(N, H * C) + h @ Wskip + bskip
        return x + jax.nn.relu(out)

    def _L0_ffn_ref(x, gamma, beta, Wr, br, W1, b1, W2, b2):
        import jax, jax.numpy as jnp
        import numpy as np
        E = 8
        K = 2
        D = 256
        H = 512
        DOUT = 256
        EPS = 1e-05
        mu = jnp.mean(x, axis=-1, keepdims=True)
        var = jnp.mean(jnp.square(x - mu), axis=-1, keepdims=True)
        xn = (x - mu) * jax.lax.rsqrt(var + EPS) * gamma + beta
        logits = jnp.einsum('bsd,de->bse', xn, Wr) + br
        top_vals, top_idx = jax.lax.top_k(logits, K)
        w = jax.nn.softmax(top_vals, axis=-1)
        w_full = jnp.einsum('bsk,bske->bse', w, jax.nn.one_hot(top_idx, E, dtype=w.dtype))
        y = jnp.zeros(x.shape[:-1] + (DOUT,), x.dtype)
        for e in range(E):
            h = jax.nn.gelu(jnp.einsum('bsd,dh->bsh', xn, W1[e]) + b1[e], approximate=False)
            y_e = jnp.einsum('bsh,hd->bsd', h, W2[e]) + b2[e]
            y = y + y_e * w_full[..., e, None]
        return y

    def _L1_gnn_ref(vertex_features, edge_index, w0, w1):
        import jax, jax.numpy as jnp
        import numpy as np
        N_NODES = 6250
        N_EDGES = 100000
        D_IN = 256
        D_OUT = 256
        w0_features = vertex_features @ w0
        w1_features = vertex_features @ w1
        dst, src = (edge_index[0], edge_index[1])
        messages = w1_features[src]
        neighbours = jax.ops.segment_sum(messages, dst, num_segments=vertex_features.shape[0])
        return jax.nn.relu(w0_features + neighbours)

    def _L1_ffn_ref(x, W_gat, att_src, att_dst, b_gat, ln_gamma, ln_beta, W1, b1, W2, b2, edge_index):
        import jax, jax.numpy as jnp
        import numpy as np
        B, N, D = (16, 512, 256)
        NUM_EXPERTS, TOP_K, HEADS = (4, 2, 4)
        N_EDGES = 131072
        LN_EPS = 1e-05

        def _layernorm(x, g, b):
            mu = x.mean(-1, keepdims=True)
            var = ((x - mu) ** 2).mean(-1, keepdims=True)
            return (x - mu) * jax.lax.rsqrt(var + LN_EPS) * g + b

        def _forward(x, edge_index, W_gat, att_src, att_dst, b_gat, ln_gamma, ln_beta, W1, b1, W2, b2):
            Bc, Nc, Dc = x.shape
            M = Bc * Nc
            x_flat = x.reshape(M, Dc)
            h = (x_flat @ W_gat).reshape(M, HEADS, NUM_EXPERTS)
            loops = jnp.arange(M, dtype=edge_index.dtype)
            src = jnp.concatenate([edge_index[0], loops])
            dst = jnp.concatenate([edge_index[1], loops])
            a_src = (h * att_src).sum(-1)
            a_dst = (h * att_dst).sum(-1)
            e = jax.nn.leaky_relu(a_src[src] + a_dst[dst], negative_slope=0.2)
            e_max = jax.ops.segment_max(e, dst, num_segments=M)
            ee = jnp.exp(e - e_max[dst])
            denom = jax.ops.segment_sum(ee, dst, num_segments=M)
            alpha = ee / (denom[dst] + 1e-16)
            msg = h[src] * alpha[:, :, None]
            agg = jax.ops.segment_sum(msg, dst, num_segments=M).reshape(M, HEADS * NUM_EXPERTS) + b_gat
            scores = _layernorm(agg, ln_gamma, ln_beta).reshape(M, HEADS, NUM_EXPERTS).mean(1)
            scores = scores.reshape(Bc, Nc, NUM_EXPERTS)
            topk_s, topk_i = jax.lax.top_k(scores, TOP_K)
            w = jax.nn.softmax(topk_s, axis=-1)
            out = jnp.zeros_like(x)
            for ei in range(NUM_EXPERTS):
                g = jnp.where(topk_i == ei, w, 0.0).sum(-1)
                hh = jax.nn.gelu(x @ W1[ei] + b1[ei], approximate=False)
                out = out + g[..., None] * (hh @ W2[ei] + b2[ei])
            return out
        return _forward(x, edge_index, W_gat, att_src, att_dst, b_gat, ln_gamma, ln_beta, W1, b1, W2, b2)

    def _L2_gnn_ref(h, w, snorm_n, edge_src, edge_dst, W_self, W_func, W_att):
        import jax, jax.numpy as jnp
        import numpy as np
        N_NODES = 1250
        N_EDGES = 20000
        IN_FEATS = 256
        E_DIMS = 64
        NEG_SLOPE = 0.01
        N = h.shape[0]
        h_s = h @ W_self.T
        z = h @ W_func.T
        concat_z = jnp.concatenate([z[edge_src], z[edge_dst], w], axis=-1)
        e = jax.nn.leaky_relu(concat_z @ W_att.T, negative_slope=NEG_SLOPE)[:, 0]
        m = jax.ops.segment_max(e, edge_dst, num_segments=N)
        e_exp = jnp.exp(e - m[edge_dst])
        denom = jax.ops.segment_sum(e_exp, edge_dst, num_segments=N)
        alpha = e_exp / denom[edge_dst]
        agg = jax.ops.segment_sum(alpha[:, None] * z[edge_src], edge_dst, num_segments=N)
        h_new = h_s + agg
        deg = jax.ops.segment_sum(jnp.ones_like(e), edge_dst, num_segments=N)
        h_new = jnp.where(deg[:, None] > 0, h_new, h)
        h_new = jax.nn.relu(h_new)
        return h + h_new

    def _L2_ffn_ref(input_embeddings, router_w, w1, b1, w2, b2):
        import jax, jax.numpy as jnp
        import numpy as np
        NUM_EXPERTS = 8
        TOP_K = 2
        B, S, D = (8, 1024, 256)

        def _moe(tokens, router_w, w1, b1, w2, b2):
            N = tokens.shape[0]
            E = router_w.shape[0]
            logits = tokens.astype(jnp.float32) @ router_w.astype(jnp.float32).T
            probs = jax.nn.softmax(logits, axis=-1)
            rw, re = jax.lax.top_k(probs, TOP_K)
            if TOP_K > 1:
                rw = rw / jnp.maximum(rw.sum(-1, keepdims=True), 1e-12)
            rw = rw.astype(tokens.dtype)
            combine = jnp.zeros((N, E), tokens.dtype).at[jnp.arange(N)[:, None], re].set(rw)
            out = tokens
            for e in range(E):
                h = jax.nn.gelu(tokens @ w1[e] + b1[e], approximate=False)
                y = h @ w2[e] + b2[e]
                out = out + combine[:, e:e + 1] * y
            return out
        b, s, d = input_embeddings.shape
        tokens = input_embeddings.reshape(b * s, d)
        return _moe(tokens, router_w, w1, b1, w2, b2).reshape(b, s, d)

    def _L3_gnn_ref(x, edge_index, weight, attn_l, attn_r):
        import jax, jax.numpy as jnp
        import numpy as np
        N, IN_CH, HEADS, OUT_CH, E = (6250, 256, 4, 64, 100000)
        heads, out_ch = attn_l.shape
        n = x.shape[0]
        xt = jnp.matmul(x, weight).reshape(-1, heads, out_ch)
        row, col = (edge_index[0], edge_index[1])
        alpha_l = jnp.einsum('ehd,hd->eh', xt[row], attn_l)
        alpha_r = jnp.einsum('ehd,hd->eh', xt[col], attn_r)
        alpha = jax.nn.softmax(jax.nn.leaky_relu(alpha_l + alpha_r, 0.01), axis=1)
        tmp = jnp.einsum('nh,nhd->nd', alpha[:n], xt[col[:n]])
        out = jnp.broadcast_to(tmp[:, None, :], (n, heads, out_ch))
        return out.reshape(n, heads * out_ch)

    def _L3_ffn_ref(h, gate_w, gate_b, w1, b1, w2, b2):
        import math
        import jax, jax.numpy as jnp
        import numpy as np
        CAPACITY_FACTOR = 1.25
        B, L, D = h.shape
        E = gate_w.shape[1]
        T = B * L
        C = max(1, math.ceil(CAPACITY_FACTOR * T / E))
        x = h.reshape(T, D)
        logits = x @ gate_w + gate_b
        probs = jax.nn.softmax(logits, axis=-1)
        idx = jnp.argmax(probs, axis=-1)
        prb = jnp.take_along_axis(probs, idx[:, None], axis=1)[:, 0]
        one_hot = jax.nn.one_hot(idx, E, dtype=jnp.float32)
        pos = (jnp.cumsum(one_hot, axis=0) * one_hot).sum(-1).astype(jnp.int32) - 1
        kept = pos < C
        pos_safe = jnp.where(kept, pos, C)
        buf = jnp.zeros((E, C, D), dtype=h.dtype).at[idx, pos_safe].set(x, mode='drop')
        hmid = jax.nn.relu(jnp.einsum('ecd,edf->ecf', buf, w1) + b1[:, None, :])
        ybuf = jnp.einsum('ecf,efd->ecd', hmid, w2) + b2[:, None, :]
        pos_g = jnp.minimum(pos, C - 1)
        y_tok = ybuf[idx, pos_g] * (prb * kept)[:, None]
        y = y_tok.reshape(B, L, D)
        y = jnp.nan_to_num(y, nan=0.0, posinf=10000.0, neginf=-10000.0)
        return y
    edge_index = jnp.stack([src, dst])
    x = x + _L0_gnn_ref(_layernorm(x, axis=-1), edge_index, L0_gnn_ln_gamma, L0_gnn_ln_beta, L0_gnn_Wq, L0_gnn_bq, L0_gnn_Wk, L0_gnn_bk, L0_gnn_Wv, L0_gnn_bv, L0_gnn_Wskip, L0_gnn_bskip)
    x = x + _L0_ffn_ref(_layernorm(x, axis=-1)[None], L0_ffn_gamma, L0_ffn_beta, L0_ffn_Wr, L0_ffn_br, L0_ffn_W1, L0_ffn_b1, L0_ffn_W2, L0_ffn_b2)[0]
    x = x + _L1_gnn_ref(_layernorm(x, axis=-1), edge_index, L1_gnn_w0, L1_gnn_w1)
    x = x + _L1_ffn_ref(_layernorm(x, axis=-1)[None], L1_ffn_W_gat, L1_ffn_att_src, L1_ffn_att_dst, L1_ffn_b_gat, L1_ffn_ln_gamma, L1_ffn_ln_beta, L1_ffn_W1, L1_ffn_b1, L1_ffn_W2, L1_ffn_b2, L1_ffn_edge_index)[0]
    x = x + _L2_gnn_ref(_layernorm(x, axis=-1), edge_attr_64, node_vec1, src, dst, L2_gnn_W_self, L2_gnn_W_func, L2_gnn_W_att)
    x = x + _L2_ffn_ref(_layernorm(x, axis=-1)[None], L2_ffn_router_w, L2_ffn_w1, L2_ffn_b1, L2_ffn_w2, L2_ffn_b2)[0]
    x = x + _L3_gnn_ref(_layernorm(x, axis=-1), edge_index, L3_gnn_weight, L3_gnn_attn_l, L3_gnn_attn_r)
    x = x + _L3_ffn_ref(_layernorm(x, axis=-1)[None], L3_ffn_gate_w, L3_ffn_gate_b, L3_ffn_w1, L3_ffn_b1, L3_ffn_w2, L3_ffn_b2)[0]
    return x

_drawn_inputs = setup_inputs


def setup_inputs(seed=0):
    import zlib

    import numpy as np

    out = dict(_drawn_inputs(seed))
    spreads = {'L0_gnn_ln_gamma': (1.0, 0.2),
     'L0_gnn_ln_beta': (0.0, 0.1),
     'L0_gnn_bq': (0.0, 0.495),
     'L0_gnn_bk': (0.0, 2.0),
     'L0_gnn_bv': (0.0, 0.1),
     'L0_gnn_bskip': (0.0, 0.1),
     'L0_ffn_br': (0.0, 0.1),
     'L1_ffn_b_gat': (0.0, 0.1),
     'L1_ffn_ln_gamma': (1.0, 0.2),
     'L1_ffn_ln_beta': (0.0, 0.1),
     'L1_ffn_b1': (0.0, 0.326),
     'L1_ffn_b2': (0.0, 0.1),
     'L2_ffn_b1': (0.0, 0.791),
     'L2_ffn_b2': (0.0, 0.522),
     'L3_ffn_gate_b': (0.0, 0.483),
     'L3_ffn_b1': (0.0, 2.0),
     'L3_ffn_b2': (0.0, 2.0)}
    factors = {'L0_ffn_gamma': 6.049,
     'L0_ffn_beta': 5.175,
     'L0_ffn_b1': 8.0,
     'L0_ffn_b2': 2.741,
     'L1_ffn_att_src': 3.27,
     'L1_ffn_att_dst': 4.781,
     'L3_ffn_w1': 2.696}
    for name, (base, spread) in spreads.items():
        noise = np.random.default_rng([zlib.crc32(name.encode()), seed]).standard_normal(out[name].shape)
        drawn = base * np.exp(spread * noise) if base else spread * noise
        out[name] = jnp.asarray(drawn.astype(out[name].dtype))
    for name, factor in factors.items():
        out[name] = (out[name] * factor).astype(out[name].dtype)
    return out
```

```python
from contextlib import ExitStack


import concourse.bass as bass
from concourse import mybir

F32 = mybir.dt.float32
BF16 = mybir.dt.bfloat16
I32 = mybir.dt.int32
U32 = mybir.dt.uint32
ALU = mybir.AluOpType
ACT = mybir.ActivationFunctionType
AX = mybir.AxisListType
ds = bass.ds

P = 128
N = 6250
D = 256
DC = D // P
T = -(-N // P)
LAST = N - (T - 1) * P
Q = 4
EPS = 1e-5
FAR = 1.0e30


class Phase:

    def __init__(self, nc, name):
        self.nc, self.name, self.ctx, self.sems = nc, name, ExitStack(), []

    def __enter__(self):
        return self

    def sb(self, name, shape, dt=F32):
        return self.ctx.enter_context(self.nc.sbuf_tensor(f"{self.name}_{name}", shape, dt))

    def ps(self, name, shape, dt=F32):
        return self.ctx.enter_context(self.nc.psum_tensor(f"{self.name}_{name}", shape, dt))

    def sem(self, name):
        s = self.ctx.enter_context(self.nc.semaphore(f"{self.name}_{name}"))
        self.sems.append(s)
        return s

    gathered = []

    def gathered_sem(self, slot):
        self.sems.append(self.gathered[slot])
        return self.gathered[slot]

    def __exit__(self, *exc):
        if exc[0] is None:
            if any(s is g for s in self.sems for g in self.gathered):
                first = self.gathered[0].num
                assert [g.num for g in self.gathered] == list(range(first, first + 4))
                self.nc.gpsimd.drain()
                self.nc.gpsimd.dma_reset(range(first, first + 4))
            for s in self.sems:
                self.nc.gpsimd.sem_clear(s)
            self.nc.all_engine_barrier()
        self.ctx.close()
        return False


def steps(eng, n, stages, lead=4, tail=0, unroll=2):
    total = n + max(lag for lag, _ in stages)
    stages = sorted(stages, key=lambda s: -s[0])

    def emit(s, slot, peeled):
        for lag, fn in stages:
            if not peeled or 0 <= s - lag < n:
                fn(s - lag, (slot - lag) % unroll)

    rounds = max(0, (n - lead - tail) // unroll)
    for s in range(min(lead, total)):
        emit(s, s % unroll, True)
    if rounds:
        with eng.Fori(0, rounds) as i:
            for k in range(unroll):
                emit(i * unroll + (lead + k), (lead + k) % unroll, False)
    for s in range(lead + unroll * rounds, total):
        emit(s, s % unroll, True)


def fixed(q):
    return isinstance(q, int)


def wait_free(eng, sem, count, q, need=1):
    if not fixed(q) or count >= need:
        eng.wait_ge(sem, count)


def bc(ap, axis, shape):
    return ap.unsqueeze(axis).to_broadcast(shape)


def make_constants(nc, core):
    with Phase(nc, "const") as ph:
        row_i = ph.sb("row_i", [P, P], I32)
        part_i = ph.sb("part_i", [P, 1], I32)
        made = ph.sem("made")
        with nc.Block() as block:
            @block.gpsimd
            def _(pool):
                pool.iota(row_i[:], pattern=[[1, P]], base=0, channel_multiplier=0).then_inc(made, 1)
                pool.iota(part_i[:], pattern=[[0, 1]], base=0, channel_multiplier=1).then_inc(made, 1)
                pool.memset(core.ident[:], 0.0).then_inc(made, 1)
                pool.memset(core.tri[:], 1.0).then_inc(made, 1)
                pool.memset(core.ones[:], 1.0).then_inc(made, 1)
                pool.wait_ge(made, 5)
                pool.affine_select(out=core.ident[:], in_=core.ident[:], compare_op=ALU.not_equal, fill=1.0,
                                   base=0, pattern=[[-1, P]], channel_multiplier=1).then_inc(made, 1)
                pool.affine_select(out=core.tri[:], in_=core.tri[:], compare_op=ALU.is_gt, fill=0.0,
                                   base=0, pattern=[[1, P]], channel_multiplier=-1).then_inc(made, 1)

            @block.vector
            def _(dve):
                dve.wait_ge(made, 7)
                dve.tensor_copy(core.row[:], row_i[:])
                dve.tensor_copy(core.part[:], part_i[:])
                dve.tensor_copy(core.ident_b[:], core.ident[:])
                for h in range(4):
                    dve.tensor_copy(core.ident4_b[:, h, :], core.ident[:])


class EdgeList:

    def __init__(self, nc, ctx, name, edges, chunk):
        self.name, self.edges, self.chunk = name, edges, chunk
        self.cols = -(-edges // P)
        self.tiles = -(-(self.cols + T) // (2 * Q)) * 2 * Q
        self.quads = self.tiles // Q
        self.dram = nc.dram_tensor(f"{name}_records", [P * self.tiles, 4], I32).ap()
        sb = lambda n, s, dt: ctx.enter_context(nc.sbuf_tensor(f"{name}_{n}", s, dt))
        self.src = sb("src", [P, self.tiles], I32)
        self.dst = sb("dst", [P, self.tiles], F32)
        self.extra = sb("extra", [P, self.tiles], F32) if name == "main" else None
        self.block = sb("block", [1, self.tiles], I32)


def sort_edges(nc, core, L, src_d, dst_d, attr_d=None, watt_d=None):
    C, CC, TE = L.cols, L.chunk, L.tiles
    assert C % CC == 0 and L.edges % 2 == 0
    full, rest = L.edges // C, L.edges % C
    with Phase(nc, f"sort_{L.name}") as ph:
        src = ph.sb("src", [P, C], I32)
        dst = ph.sb("dst", [P, C], I32)
        di = ph.sb("di", [P, C], I32)
        buck = ph.sb("buck", [P, C])
        far = ph.sb("far", [P, C])
        rl = ph.sb("rl", [P, C])
        rec = ph.sb("rec", [P, C, 4], I32)
        recf = rec[:].bitcast(F32)
        rows = ph.sb("rows", [P, C], I32)
        fill = ph.sb("fill", [P, TE, 4], I32)
        oh = ph.sb("oh", [P, T, CC + 1])
        rk = ph.sb("rk", [P, T, CC + 1])
        keep = ph.sb("keep", [P, T, CC + 1])
        base = ph.sb("base", [P, T])
        cnt = ph.sb("cnt", [P, T])
        nt = ph.sb("nt", [P, T])
        nti = ph.sb("nti", [P, T], I32)
        endt = ph.sb("endt", [P, T])
        one_t = ph.sb("one_t", [P, T])
        ntc = ph.sb("ntc", [T, 2])
        ntci = ph.sb("ntci", [T, 1], I32)
        slot_i = ph.sb("slot_i", [T, TE], I32)
        cmp = ph.sb("cmp", [T, TE])
        blkf = ph.sb("blkf", [1, TE])
        tri_inc = ph.sb("tri_inc", [T, T])
        stage_rec = ph.sb("stage_rec", [P, 2, Q * 4], I32)
        stage_row = ph.sb("stage_row", [P, 2, Q], I32)
        sums = ph.ps("sums", [P, 2, T])
        col = ph.ps("col", [T, 2])
        blk = ph.ps("blk", [1, 3, 512])
        listed, filled, d, placed, tot, colsum, colend, blksum, slots, nothing, staged, stored, attr_in, ewd = [
            ph.sem(n) for n in ("listed", "filled", "dve", "placed", "tot", "colsum", "colend", "blksum", "slots",
                                "nothing", "staged", "stored", "attr_in", "attr_done")]
        taken = ph.sem("taken")
        freed = [ph.gathered_sem(k) for k in range(2)]
        AC = 23 if attr_d is not None else 0
        if attr_d is not None:
            attr = ph.sb("attr", [P, 2, AC, 64])
            w3 = ph.sb("w3", [P, 64])
            att_sem = [ph.sem("attr0"), ph.sem("attr1")]
            attr_t = attr_d[L.edges - C:L.edges, :].rearrange("(o c) k -> o c k", o=1)
            attr_v = attr_d[0:full * C, :].rearrange("(p c) k -> p c k", c=C)
        nblk = -(-TE // 512)
        bw = TE // nblk
        assert bw * nblk == TE and bw <= 512
        cols_q = -(-C // Q)

        with nc.Block() as block:
            @block.sync
            def _(sp):
                for v, a, first in ((src_d, src, 0), (dst_d, dst, C - rest if rest else 0)):
                    if a is dst:
                        sp.wait_ge(nothing, 1)
                    sp.dma_start(a[0:full, :], v[0:full * C].rearrange("(p c) -> p c", c=C)).then_inc(listed, 16)
                    if rest:
                        sp.dma_start(a[full:full + 1, first:C], v[L.edges - C + first:L.edges]
                                     .rearrange("(o c) -> o c", o=1)).then_inc(listed, 16)
                if attr_d is not None:
                    sp.dma_start(w3[:], watt_d[0:1, 2 * D:2 * D + 64].to_broadcast([P, 64])).then_inc(attr_in, 16)

                    def load(q, par):
                        wait_free(sp, ewd, q * 2 - 2, q, 2)
                        sp.dma_start(attr[0:full, par], attr_v[:, ds(q * AC, AC), :]).then_inc(att_sem[par], 16)
                        sp.dma_start(attr[full:full + 1, par], attr_t[:, ds(q * AC, AC), :]).then_inc(att_sem[par], 16)
                    steps(sp, C // AC, [(0, load)])
                sp.wait_ge(filled, 1)
                sp.dma_start(L.dram.rearrange("(p t) k -> p (t k)", p=P),
                             fill[:].rearrange("p t k -> p (t k)")).then_inc(placed, 16)
                for par in range(2):
                    sp.wait_ge(freed[par], 16 * sum(min(Q, C - Q * q) for q in range(par, cols_q, 2)))
                sp.dma_start(fill[:].rearrange("p t k -> p (t k)"),
                             L.dram.rearrange("(p t) k -> p (t k)", p=P)).then_inc(slots, 16)

            @block.vector
            def _(dve):
                n = [0]

                def done(ins):
                    n[0] += 1
                    ins.then_inc(d, 1)
                    dve.wait_ge(d, n[0])

                dve.memset(dst[:], 1 << 20).then_inc(nothing, 1)
                done(dve.memset(keep[:], 1.0))
                done(dve.memset(keep[:, :, 0:1], 0.0))
                done(dve.memset(oh[:], 0.0))
                done(dve.memset(rk[:], 0.0))
                done(dve.memset(one_t[:], 1.0))
                done(dve.memset(rec[:], 0))
                done(dve.memset(fill[:], 0))
                fillf = fill[:].bitcast(F32)
                dve.memset(fillf[:, :, 1:2], -1.0).then_inc(filled, 1)
                dve.wait_ge(listed, 64 if rest else 32)
                done(dve.tensor_scalar(di[:], dst[:], 7, None, ALU.logical_shift_right))
                done(dve.tensor_copy(buck[:], di[:]))
                done(dve.tensor_copy(far[:], dst[:]))
                done(dve.tensor_scalar(far[:], far[:], float(N), 1.0e7, ALU.is_ge, ALU.mult))
                done(dve.tensor_tensor(buck[:], buck[:], far[:], ALU.add))
                done(dve.tensor_scalar(rec[:, :, 0], src[:], N - 1, None, ALU.min))
                done(dve.tensor_scalar(di[:], dst[:], P - 1, None, ALU.bitwise_and))
                done(dve.tensor_copy(recf[:, :, 1], di[:]))
                if attr_d is not None:
                    dve.wait_ge(attr_in, 16)

                    def edge_score(q, par):
                        dve.wait_ge(att_sem[par], (q - par) * 16 + 32)
                        dve.tensor_tensor(attr[:, par], attr[:, par], bc(w3[:], 1, [P, AC, 64]),
                                          ALU.mult).then_inc(ewd, 1)
                        dve.wait_ge(ewd, q * 2 + 1)
                        dve.tensor_reduce(recf[:, ds(q * AC, AC), 2], attr[:, par], AX.X, ALU.add).then_inc(ewd, 1)
                    steps(dve, C // AC, [(0, edge_score)])
                n0 = n[0]
                with dve.Fori(0, C // CC) as i:
                    c = lambda k: i * 5 + (n0 + k)
                    dve.tensor_tensor(oh[:, :, 1:], bc(buck[:, ds(i * CC, CC)], 1, [P, T, CC]),
                                      bc(core.row[:, 0:T], 2, [P, T, CC]), ALU.is_equal).then_inc(d, 1)
                    dve.tensor_copy(oh[:, :, 0:1], rk[:, :, CC:CC + 1]).then_inc(d, 1)
                    dve.wait_ge(d, c(2))
                    dve.tensor_tensor_scan(rk[:].rearrange("p b c -> p (b c)"), keep[:].rearrange("p b c -> p (b c)"),
                                           oh[:].rearrange("p b c -> p (b c)"), 0.0, ALU.mult, ALU.add).then_inc(d, 1)
                    dve.wait_ge(d, c(3))
                    dve.tensor_tensor(oh[:, :, 1:], oh[:, :, 1:], rk[:, :, 1:], ALU.mult).then_inc(d, 1)
                    dve.wait_ge(d, c(4))
                    dve.tensor_reduce(rl[:, ds(i * CC, CC)], oh[:, :, 1:].rearrange("p b c -> p c b"),
                                      AX.X, ALU.add).then_inc(d, 1)
                    dve.wait_ge(d, c(5))
                n[0] += 5 * (C // CC)
                dve.tensor_copy(cnt[:], rk[:, :, CC]).then_inc(tot, 1)
                dve.wait_ge(colsum, 2)
                done(dve.tensor_scalar(nt[:], sums[:, 1, :], P - 1.0, None, ALU.add))
                done(dve.tensor_copy(nti[:], nt[:]))
                done(dve.tensor_scalar(nti[:], nti[:], 7, None, ALU.logical_shift_right))
                done(dve.tensor_copy(nt[:], nti[:]))
                done(dve.tensor_tensor_scan(endt[:], one_t[:], nt[:], 0.0, ALU.mult, ALU.add))
                done(dve.tensor_tensor(base[:], endt[:], nt[:], ALU.subtract))
                done(dve.tensor_scalar(base[:], base[:], float(P), -1.0, ALU.mult, ALU.add))
                done(dve.tensor_tensor(base[:], base[:], sums[:, 0, :], ALU.add))
                done(dve.tensor_scalar(ntc[:, 0:1], col[:, 0:1], P - 1.0, None, ALU.add))
                done(dve.tensor_copy(ntci[:], ntc[:, 0:1]))
                done(dve.tensor_scalar(ntci[:], ntci[:], 7, None, ALU.logical_shift_right))
                done(dve.tensor_tensor(tri_inc[:], core.tri[0:T, 0:T], core.ident[0:T, 0:T], ALU.add))
                dve.tensor_copy(ntc[:, 0:1], ntci[:]).then_inc(tot, 1)
                dve.wait_ge(colend, 1)
                done(dve.tensor_copy(ntc[:, 1:2], col[:, 1:2]))
                dve.wait_ge(slots, 1)
                done(dve.tensor_copy(cmp[:], slot_i[:]))
                dve.tensor_scalar(cmp[:], cmp[:], ntc[:, 1:2], None, ALU.is_ge).then_inc(tot, 1)
                dve.wait_ge(blksum, 1)
                done(dve.tensor_scalar(blkf[:].rearrange("o (a b) -> o a b", a=nblk), blk[:, 0:nblk, 0:bw],
                                       T - 1.0, None, ALU.min))
                done(dve.tensor_copy(L.block[:], blkf[:]))
                n1 = n[0]
                with dve.Fori(0, C // CC) as i:
                    c = lambda k: i * 4 + (n1 + k)
                    dve.tensor_tensor(oh[:, :, 1:], bc(buck[:, ds(i * CC, CC)], 1, [P, T, CC]),
                                      bc(core.row[:, 0:T], 2, [P, T, CC]), ALU.is_equal).then_inc(d, 1)
                    dve.wait_ge(d, c(1))
                    dve.tensor_tensor(oh[:, :, 1:], oh[:, :, 1:], bc(base[:], 2, [P, T, CC]), ALU.mult).then_inc(d, 1)
                    dve.wait_ge(d, c(2))
                    dve.tensor_reduce(rk[:, 0, 0:CC], oh[:, :, 1:].rearrange("p b c -> p c b"),
                                      AX.X, ALU.add).then_inc(d, 1)
                    dve.wait_ge(d, c(3))
                    dve.tensor_tensor(rl[:, ds(i * CC, CC)], rl[:, ds(i * CC, CC)], rk[:, 0, 0:CC],
                                      ALU.add).then_inc(d, 1)
                    dve.wait_ge(d, c(4))
                n[0] += 4 * (C // CC)
                done(dve.tensor_copy(di[:], rl[:]))
                done(dve.tensor_scalar(dst[:], di[:], P - 1, None, ALU.bitwise_and))
                done(dve.tensor_scalar(di[:], di[:], 7, None, ALU.logical_shift_right))
                done(dve.tensor_copy(buck[:], dst[:]))
                done(dve.tensor_copy(rl[:], di[:]))
                done(dve.scalar_tensor_tensor(out=rl[:], in0=buck[:], scalar=float(TE), in1=rl[:],
                                              op0=ALU.mult, op1=ALU.add))
                done(dve.tensor_tensor(rl[:], rl[:], far[:], ALU.add))
                dve.tensor_copy(rows[:], rl[:]).then_inc(tot, 1)
                dve.wait_ge(slots, 17)
                dve.tensor_copy(L.src[:], fill[:, :, 0])
                dve.tensor_copy(L.dst[:], fillf[:, :, 1])
                if L.extra is not None:
                    dve.tensor_copy(L.extra[:], fillf[:, :, 2])

            @block.tensor
            def _(pe):
                pe.wait_ge(tot, 1)
                pe.matmul(sums[:, 0, :], core.tri[:], cnt[:], start=True, stop=True)
                pe.matmul(sums[:, 1, :], core.ones[:], cnt[:], start=True, stop=True).then_inc(colsum, 1)
                pe.matmul(col[:, 0:1], cnt[:], core.ones[:, 0:1], start=True, stop=True).then_inc(colsum, 1)
                pe.wait_ge(tot, 2)
                pe.matmul(col[:, 1:2], tri_inc[:], ntc[:, 0:1], start=True, stop=True).then_inc(colend, 1)
                pe.wait_ge(tot, 3)
                for k in range(nblk):
                    ins = pe.matmul(blk[:, k, 0:bw], core.ones[0:T, 0:1], cmp[:, k * bw:(k + 1) * bw],
                                    start=True, stop=True)
                ins.then_inc(blksum, 1)

            @block.scalar
            def _(act):
                act.wait_ge(tot, 4)

                def stage(q, par):
                    wait_free(act, freed[par], (q - par) * (8 * Q), q)
                    w = min(Q, C - Q * q) if fixed(q) else Q
                    act.copy(stage_rec[:, par, 0:4 * w], rec[:, ds(q * Q, w), :].rearrange("p c k -> p (c k)"))
                    act.copy(stage_row[:, par, 0:w], rows[:, ds(q * Q, w)]).then_inc(staged, 1)
                steps(act, cols_q, [(0, stage)], tail=1)

            @block.gpsimd
            def _(pool):
                pool.iota(slot_i[:], pattern=[[1, TE]], base=0, channel_multiplier=0).then_inc(slots, 1)
                pool.wait_ge(placed, 16)
                bound = pool.to_reg(P * TE - 1)

                def store(q, par):
                    pool.wait_ge(staged, q + 1)
                    pool.sem_inc(taken, 1)
                    w = min(Q, C - Q * q) if fixed(q) else Q
                    for j in range(w):
                        pool.indirect_dma_start(
                            L.dram, bass.IndirectOffsetOnAxis(ap=stage_row[:, par, j:j + 1], axis=0),
                            stage_rec[:, par, 4 * j:4 * j + 4], None,
                            bounds_check=bound, oob_is_err=False).then_inc(freed[par], 16)
                steps(pool, cols_q, [(0, store)], tail=1)


class Own:

    def __init__(self, eng, sem, per, base=0):
        self.eng, self.sem, self.per, self.base = eng, sem, per, base

    def at(self, q):
        self.first, self.k = q * self.per + self.base, 0
        return self

    def mark(self, ins):
        self.k += 1
        ins.then_inc(self.sem, 1)
        assert self.k <= self.per

    def then(self, ins):
        self.mark(ins)
        self.eng.wait_ge(self.sem, self.first + self.k)


def copy_f(dve, out, in_):
    return dve.tensor_scalar(out, in_, 1.0, None, ALU.mult)


def rows_of(table, t, a=0, b=None):
    return table[ds(t * P, P), a:(table.shape[1] if b is None else b)]


def statistics(nc, core, inp, name):
    with Phase(nc, name) as ph:
        st = ph.sb("st", [P, T, 6])
        half = ph.sb("half", [P, T])
        mean = ph.sb("mean", [P, T])
        ve = ph.sb("ve", [P, T])
        sq = ph.sb("sq", [P, T])
        stat, own2, sq_ready = [ph.sem(n) for n in ("stat", "rest", "sq_ready")]
        with nc.Block() as block:
            @block.vector
            def _(dve):
                with dve.Fori(0, T) as t:
                    dve.bn_stats(st[:, ds(t, 1), :].rearrange("p o d -> p (o d)"),
                                 inp[:, ds(t, 1), :].rearrange("p o d -> p (o d)")).then_inc(stat, 1)
                dve.wait_ge(stat, T)
                o = Own(dve, own2, 16).at(0)
                o.then(dve.tensor_tensor(half[:], st[:, :, 1], st[:, :, 4], ALU.subtract))
                o.then(dve.tensor_scalar(half[:], half[:], 0.5, None, ALU.mult))
                o.then(dve.tensor_tensor(half[:], half[:], half[:], ALU.mult))
                o.then(dve.tensor_tensor(mean[:], st[:, :, 1], st[:, :, 4], ALU.add))
                o.then(dve.tensor_scalar(mean[:], mean[:], 0.5, None, ALU.mult))
                o.then(dve.tensor_tensor(ve[:], st[:, :, 2], st[:, :, 5], ALU.add))
                o.then(dve.scalar_tensor_tensor(out=ve[:], in0=ve[:], scalar=1.0 / D, in1=half[:],
                                                op0=ALU.mult, op1=ALU.add))
                o.mark(dve.tensor_scalar(ve[:], ve[:], EPS, None, ALU.add))
                dve.wait_ge(sq_ready, 1)
                o.then(dve.reciprocal(core.rstd[:], sq[:]))
                o.then(dve.tensor_tensor(half[:], core.rstd[:], core.rstd[:], ALU.mult))
                o.then(dve.tensor_tensor(half[:], half[:], ve[:], ALU.mult))
                o.then(dve.tensor_scalar(half[:], half[:], -0.5, 1.5, ALU.mult, ALU.add))
                o.then(dve.tensor_tensor(core.rstd[:], core.rstd[:], half[:], ALU.mult))
                o.then(dve.scalar_tensor_tensor(out=core.nmean[:], in0=mean[:], scalar=-1.0, in1=core.rstd[:],
                                                op0=ALU.mult, op1=ALU.mult))

            @block.scalar
            def _(act):
                act.wait_ge(own2, 8)
                act.activation(sq[:], ve[:], ACT.Sqrt).then_inc(sq_ready, 1)


def normalize(nc, core, out, name, add=True):
    with Phase(nc, name) as ph:
        z_ready = ph.sem("z_ready")
        with nc.Block() as block:
            @block.scalar
            def _(act):
                def scale(t, par):
                    act.activation(out[:, ds(t, 1), :].rearrange("p o d -> p (o d)"),
                                   core.x[:, ds(t, 1), :].rearrange("p o d -> p (o d)"), ACT.Identity,
                                   bias=core.nmean[:, ds(t, 1)], scale=core.rstd[:, ds(t, 1)]).then_inc(z_ready, 1)
                steps(act, T, [(0, scale)])

            if add:
                @block.vector
                def _(dve):
                    def add_z(t, par):
                        dve.wait_ge(z_ready, t + 1)
                        dve.tensor_tensor(core.x[:, ds(t, 1), :], core.x[:, ds(t, 1), :], out[:, ds(t, 1), :],
                                          ALU.add)
                    steps(dve, T, [(0, add_z)])


def load_transposed(nc, core, parts, name):
    with Phase(nc, name) as ph:
        raw = ph.sb("raw", [P, 2 * len(parts), D])
        tp = ph.ps("tp", [P, 2, 512])
        got, turned, copied = [ph.sem(n) for n in ("got", "turned", "copied")]
        pieces = []
        for k, (dst, w) in enumerate(parts):
            for r in range(-(-w.shape[0] // P)):
                pieces.append((2 * k + r, dst, w, r * P, min(P, w.shape[0] - r * P)))
        with nc.Block() as block:
            @block.sync
            def _(sp):
                for k, dst, w, r0, n in pieces:
                    sp.dma_start(raw[0:n, k, :], w[r0:r0 + n, :]).then_inc(got, 16)

            @block.tensor
            def _(pe):
                pe.wait_ge(got, 16 * len(pieces))
                i = 0
                for k, dst, w, r0, n in pieces:
                    for c in range(DC):
                        if i >= 2:
                            pe.wait_ge(copied, i - 1)
                        pe.transpose(tp[:, i % 2, 0:n], raw[0:n, k, c * P:(c + 1) * P],
                                     core.ident[0:n, 0:n]).then_inc(turned, 1)
                        i += 1

            @block.scalar
            def _(act):
                i = 0
                for k, dst, w, r0, n in pieces:
                    for c in range(DC):
                        act.wait_ge(turned, i + 1)
                        act.copy(dst[:, c, r0:r0 + n], tp[:, i % 2, 0:n]).then_inc(copied, 1)
                        i += 1


def project(nc, core, name, inp, nout, w_loads, w_sb=None, bias_loads=(), affine=None, add_to_x=False,
            stores=(), keep_z=None, to_sbuf=(), att=(), att_loads=()):
    with Phase(nc, name) as ph:
        W = w_sb if w_sb is not None else ph.sb("w", [P, DC, nout])
        zs = ph.sb("zs", [P, 2, D])
        zt = ph.sb("zt", [P, 2, DC, P])
        osb = ph.sb("osb", [P, 2, nout])
        banks = -(-nout // 512)
        bw = nout // banks
        ztp = ph.ps("ztp", [P, 2, 512])
        op = ph.ps("op", [P, 2, banks, 512])
        bias = ph.sb("bias", [P, nout]) if bias_loads else None
        gb = ph.sb("gb", [P, 2, D]) if affine else None
        attw = ph.sb("attw", [P, len(att), D]) if att else None
        prod = ph.sb("prod", [P, 2, D]) if att else None
        (loaded, z_raw, aff, z_ready, turned, zt_ready, out_done, evac, own_att, sbuf_done, xadd) = [
            ph.sem(n) for n in ("loaded", "z_raw", "affine", "z_ready", "turned", "zt_ready", "out_done", "evac",
                                "own_att", "sbuf_done", "xadd")]
        st = [ph.sem("stored0"), ph.sem("stored1")]
        per_store = 16 * len(stores)
        n_loads = [0]
        zsem, zper = (aff, 2) if affine else (z_raw, 1)

        with nc.Block() as block:
            @block.sync
            def _(sp):
                def ld(dst, src):
                    sp.dma_start(dst, src).then_inc(loaded, 16)
                    n_loads[0] += 1
                for c0, w in w_loads:
                    ld(W[:, :, c0:c0 + w.shape[1]], w.rearrange("(c p) n -> p c n", p=P))
                for c0, v in bias_loads:
                    ld(bias[:, c0:c0 + v.shape[0]], v.rearrange("(o n) -> o n", o=1).to_broadcast([P, v.shape[0]]))
                if affine:
                    for k, v in enumerate(affine):
                        ld(gb[:, k, :], v.rearrange("(o n) -> o n", o=1).to_broadcast([P, D]))
                for k, v in att_loads:
                    ld(attw[:, k, 0:v.shape[1]], v.to_broadcast([P, v.shape[1]]))

                def store(t, par):
                    sp.wait_ge(evac, t + 1)
                    if att:
                        sp.wait_ge(own_att, (t + 1) * 2 * len(att))
                    for table, what, a, b, c0 in stores:
                        if isinstance(what, str):
                            src = zs[:, par, a:b] if what == "z" else osb[:, par, a:b]
                        else:
                            src = what[:, ds(t, 1), a:b].rearrange("p o d -> p (o d)")
                        sp.dma_start(rows_of(table, t, c0, c0 + b - a), src).then_inc(st[par], 16)
                if stores:
                    steps(sp, T, [(0, store)])
                    sp.wait_ge(st[0], per_store * ((T + 1) // 2))
                    sp.wait_ge(st[1], per_store * (T // 2))

            @block.scalar
            def _(act):
                def scale(t, par):
                    wait_free(act, turned, t - 1, t)
                    if keep_z is not None or add_to_x:
                        wait_free(act, xadd, t - 1, t)
                    if any(isinstance(s[1], str) and s[1] == "z" for s in stores):
                        wait_free(act, st[par], (t - par) * (per_store // 2), t)
                    act.activation(zs[:, par, :], inp[:, ds(t, 1), :].rearrange("p o d -> p (o d)"), ACT.Identity,
                                   bias=core.nmean[:, ds(t, 1)], scale=core.rstd[:, ds(t, 1)]).then_inc(z_raw, 1)

                def copy_t(t, par):
                    act.wait_ge(turned, t + 1)
                    wait_free(act, out_done, t - 1, t)
                    act.copy(zt[:, par].rearrange("p c k -> p (c k)"), ztp[:, par, 0:DC * P]).then_inc(zt_ready, 1)

                def to_sb(t, par):
                    act.wait_ge(evac, t + 1)
                    for k, (dst, c0) in enumerate(to_sbuf):
                        ins = act.copy(dst[:, ds(t, 1), :].rearrange("p o d -> p (o d)"),
                                       osb[:, par, c0:c0 + dst.shape[2]])
                    ins.then_inc(sbuf_done, 1)
                stages = [(0, scale), (1, copy_t)]
                if to_sbuf:
                    stages.append((2, to_sb))
                steps(act, T, stages)

            @block.tensor
            def _(pe):
                pe.wait_ge(loaded, 16 * n_loads[0])

                def turn(t, par):
                    pe.wait_ge(zsem, (t + 1) * zper)
                    wait_free(pe, zt_ready, t - 1, t)
                    for c in range(DC):
                        ins = pe.transpose(ztp[:, par, c * P:(c + 1) * P], zs[:, par, c * P:(c + 1) * P],
                                           core.ident[:])
                    ins.then_inc(turned, 1)

                def multiply(t, par):
                    pe.wait_ge(zt_ready, t + 1)
                    wait_free(pe, evac, t - 1, t)
                    for b in range(banks):
                        for c in range(DC):
                            ins = pe.matmul(op[:, par, b, 0:bw], zt[:, par, c, :], W[:, c, b * bw:(b + 1) * bw],
                                            start=(c == 0), stop=(c == DC - 1))
                    ins.then_inc(out_done, 1)
                steps(pe, T, [(0, turn), (1, multiply)])

            @block.vector
            def _(dve):
                dve.wait_ge(loaded, 16 * n_loads[0])
                assert len(att) in (0, 2)
                oa = Own(dve, own_att, 2 * len(att)) if att else None
                of = Own(dve, aff, 2)

                def finish_z(t, par):
                    dve.wait_ge(z_raw, t + 1)
                    if affine:
                        of.at(t)
                        of.then(dve.tensor_tensor(zs[:, par, :], zs[:, par, :], gb[:, 0, :], ALU.mult))
                        of.then(dve.tensor_tensor(zs[:, par, :], zs[:, par, :], gb[:, 1, :], ALU.add))
                    ins = None
                    zq = zs[:, par, :].unsqueeze(1)
                    if add_to_x:
                        ins = dve.tensor_tensor(core.x[:, ds(t, 1), :], core.x[:, ds(t, 1), :], zq, ALU.add)
                    if keep_z is not None:
                        ins = copy_f(dve, keep_z[:, ds(t, 1), :], zq)
                    if ins is not None:
                        ins.then_inc(xadd, 1)

                def evacuate(t, par):
                    dve.wait_ge(out_done, t + 1)
                    if stores:
                        wait_free(dve, st[par], (t - par) * (per_store // 2), t)
                    if to_sbuf:
                        wait_free(dve, sbuf_done, t - 1, t)
                    src = op[:, par, :, 0:bw]
                    dst = osb[:, par, :].rearrange("p (b w) -> p b w", b=banks)
                    if bias is not None:
                        dve.tensor_tensor(dst, src, bias[:].rearrange("p (b w) -> p b w", b=banks),
                                          ALU.add).then_inc(evac, 1)
                    else:
                        dve.tensor_copy(dst, src).then_inc(evac, 1)
                    if att:
                        oa.at(t)
                        dve.wait_ge(evac, t + 1)
                        for k, (dst, c0, heads, width) in enumerate(att):
                            wait_free(dve, own_att, oa.first + (2 * k - 2), t, 1)
                            a = prod[:, k % 2, 0:heads * width]
                            oa.then(dve.tensor_tensor(a, osb[:, par, c0:c0 + heads * width],
                                                      attw[:, k, 0:heads * width], ALU.mult))
                            oa.mark(dve.tensor_reduce(dst[:, ds(t, 1), :].rearrange("p o d -> p (o d)"),
                                                      a.rearrange("p (h w) -> p h w", h=heads), AX.X, ALU.add))
                steps(dve, T, [(0, finish_z), (1, evacuate)])


G4 = 4


def gather_quad(pool, table, ix, rows, sem, bound):
    for j in range(Q):
        pool.indirect_dma_start(rows[:, j, :], None, table, bass.IndirectOffsetOnAxis(ap=ix[:, j:j + 1], axis=0),
                                bounds_check=bound, oob_is_err=False).then_inc(sem, 16)


def blocks_of(nc, engine, L, q):
    _, vals = nc.values_load_multi_w_load_instructions(L.block[0:1, ds(q * Q, Q)], engines=(engine,),
                                                       min_val=0, max_val=T - 1,
                                                       skip_runtime_bounds_check_because="made below T on chip")
    return vals


def edge_max(nc, core, L, name, heads, table, width, val, best, queries=None, extra=None, kept=None):
    H, W, dot = heads, width, queries is not None
    with Phase(nc, name) as ph:
        ix = ph.sb("ix", [P, G4, Q], I32)
        rows = ph.sb("rows", [P, G4, Q, W])
        parts = ph.sb("parts", [P, 2, P], BF16)
        rem = ph.sb("rem", [P, 2, Q * H])
        far = ph.sb("far", [P, 2, Q, P], BF16)
        pt = ph.sb("pt", [P, 2, P], BF16)
        sel = ph.sb("sel", [P, Q * H, P], BF16)
        top = ph.sb("top", [P, Q, H])
        ptp = ph.ps("ptp", [P, P], BF16)
        mx = ph.ps("mx", [P, 4, 512])
        (made, ix_ready, taken, val_own, val_ready, parts_own, far_ready, pt_turned, pt_ready, mx_done, top_own,
         upd_own, s_ready, st_turned, st_ready, q_done, prod_own) = [ph.sem(n) for n in (
             "made", "ix_ready", "taken", "val_own", "val_ready", "parts_own", "far_ready", "pt_turned", "pt_ready",
             "mx_done", "top_own", "upd_own", "s_ready", "st_turned", "st_ready", "q_done", "prod_own")]
        zeroed = ph.sem("zeroed")
        got = [ph.gathered_sem(k) for k in range(G4)]
        if dot:
            s4 = ph.sb("s4", [P, 2, Q, P])
            st = ph.sb("st", [P, 2, Q, P])
            prod = ph.sb("prod", [P, Q, W])
            stp = ph.ps("stp", [P, Q, P])
            qe = ph.ps("qe", [P, Q, W])
        n = L.quads
        with nc.Block() as block:
            @block.gpsimd
            def _(pool):
                pool.memset(sel[:], 0.0).then_inc(made, 1)
                for k in range(3):
                    pool.wait_ge(made, k + 1)
                    pool.affine_select(out=sel[:], in_=sel[:], compare_op=ALU.not_equal, fill=1.0,
                                       base=-k * Q * H, pattern=[[-1, Q * H], [0, P]],
                                       channel_multiplier=1).then_inc(made, 1)
                bound = pool.to_reg(N - 1)

                def gather(q, slot):
                    wait_free(pool, val_ready, q - (G4 - 1), q)
                    pool.wait_ge(ix_ready, q + 1)
                    pool.sem_inc(taken, 1)
                    gather_quad(pool, table, ix[:, slot], rows[:, slot], got[slot], bound)
                steps(pool, n, [(0, gather)], unroll=G4, lead=8)

            @block.scalar
            def _(act):
                def index(q, slot):
                    wait_free(act, got[slot], (q - slot) * (16 * Q // G4), q)
                    act.copy(ix[:, slot, :], L.src[:, ds(q * Q, Q)]).then_inc(ix_ready, 1)

                def copy_st(q, slot):
                    act.wait_ge(st_turned, q + 1)
                    wait_free(act, q_done, q - 1, q)
                    act.copy(st[:, slot % 2], stp[:]).then_inc(st_ready, 1)

                def copy_pt(q, slot):
                    act.wait_ge(pt_turned, q + 1)
                    wait_free(act, mx_done, (q - 1) * Q, q)
                    act.copy(pt[:, slot % 2, :], ptp[:]).then_inc(pt_ready, 1)
                steps(act, n, [(0, index)] + [(1, copy_st)] * dot + [(3, copy_pt)], unroll=G4, lead=8)

            @block.tensor
            def _(pe):
                pe.wait_ge(made, 4)

                def turn_s(q, slot):
                    pe.wait_ge(s_ready, (q + 1) * Q)
                    wait_free(pe, st_ready, q, q)
                    for j in range(Q):
                        ins = pe.transpose(stp[:, j, :], s4[:, slot % 2, j, :], core.ident[:])
                    ins.then_inc(st_turned, 1)

                def query(q, slot):
                    b = blocks_of(nc, mybir.EngineType.PE, L, q)
                    pe.wait_ge(st_ready, q + 1)
                    wait_free(pe, prod_own, q, q)
                    for j in range(Q):
                        ins = pe.matmul(qe[:, j, :], st[:, slot % 2, j, :],
                                        queries[:, ds(b[j], 1), :].rearrange("p o d -> p (o d)"),
                                        start=True, stop=True)
                    ins.then_inc(q_done, 1)

                def turn_parts(q, slot):
                    pe.wait_ge(parts_own, (q + 1) * 5)
                    wait_free(pe, pt_ready, q, q)
                    pe.transpose(ptp[:], parts[:, slot % 2, :],
                                 core.ident_b[:]).then_inc(pt_turned, 1)

                def spread(q, slot):
                    pe.wait_ge(pt_ready, q + 1)
                    pe.wait_ge(far_ready, (q + 1) * Q)
                    for j in range(Q):
                        if H == 1:
                            out = mx[:, slot % 2, j * P:(j + 1) * P]
                            if j == 0:
                                wait_free(pe, top_own, q - 1, q)
                        else:
                            out = mx[:, j, 0:H * P]
                            wait_free(pe, top_own, q * Q + (j - Q + 1), q)
                        pe.matmul(out, far[:, slot % 2, j, :], core.ident4_b[:, 0:H, :].rearrange("p h k -> p (h k)"),
                                  start=True, stop=False, skip_group_check=True)
                        for h in range(H):
                            ins = pe.matmul(out[:, h * P:(h + 1) * P], sel[:, j * H + h, :], pt[:, slot % 2, :],
                                            start=False, stop=(h == H - 1), skip_group_check=True)
                        ins.then_inc(mx_done, 1)
                steps(pe, n, [(0, turn_s), (1, query)] * dot + [(2, turn_parts), (3, spread)], unroll=G4, lead=8)

            @block.vector
            def _(dve):
                op = Own(dve, parts_own, 5)
                dve.memset(parts[:], 0.0).then_inc(zeroed, 1)
                dve.wait_ge(zeroed, 1)

                def onehot(q, slot):
                    wait_free(dve, st_turned, q - 1, q)
                    for j in range(Q):
                        dve.tensor_scalar(s4[:, slot % 2, j, :], core.row[:], L.dst[:, ds(q * Q + j, 1)], None,
                                          ALU.is_equal).then_inc(s_ready, 1)

                def score(q, slot):
                    dve.wait_ge(got[slot], (q - slot) * (16 * Q // G4) + 16 * Q)
                    out = val[:, ds(q * Q, Q), :]
                    if dot:
                        dve.wait_ge(q_done, q + 1)
                        dve.tensor_tensor(prod[:], rows[:, slot], qe[:], ALU.mult).then_inc(prod_own, 1)
                        dve.wait_ge(prod_own, q + 1)
                        dve.tensor_reduce(out, prod[:].rearrange("p q (h c) -> p q h c", h=H), AX.X,
                                          ALU.add).then_inc(val_ready, 1)
                    else:
                        if kept is not None:
                            copy_f(dve, kept[:, ds(q * Q, Q), :], rows[:, slot]).then_inc(val_ready, 1)
                        elif extra is not None:
                            dve.tensor_tensor(out, rows[:, slot, :, 0:H],
                                              extra[:, ds(q * Q, Q)].unsqueeze(2), ALU.add).then_inc(val_ready, 1)
                        else:
                            copy_f(dve, out, rows[:, slot, :, 0:H]).then_inc(val_ready, 1)
                    dve.wait_ge(val_ready, q + 1)

                def split(q, slot):
                    op.at(q)
                    v = val[:, ds(q * Q, Q), :]
                    sh = lambda ap: ap.rearrange("p (q h) -> p q h", h=H)
                    hi, mid, lo = (sh(parts[:, slot % 2, k * Q * H:(k + 1) * Q * H]) for k in range(3))
                    r = sh(rem[:, slot % 2, :])
                    wait_free(dve, pt_turned, q - 1, q)
                    op.then(copy_f(dve, hi, v))
                    op.then(dve.tensor_tensor(r, v, hi, ALU.subtract))
                    op.then(dve.tensor_copy(mid, r))
                    op.then(dve.tensor_tensor(r, r, mid, ALU.subtract))
                    op.mark(dve.tensor_copy(lo, r))

                def exclude(q, slot):
                    wait_free(dve, mx_done, q * Q - Q, q)
                    for j in range(Q):
                        dve.tensor_scalar(far[:, slot % 2, j, :], core.row[:], L.dst[:, ds(q * Q + j, 1)], -FAR,
                                          ALU.not_equal, ALU.mult).then_inc(far_ready, 1)

                def update(q, slot):
                    b = blocks_of(nc, mybir.EngineType.DVE, L, q)
                    wait_free(dve, upd_own, q * Q, q)
                    if H == 1:
                        dve.wait_ge(mx_done, q * Q + Q)
                        dve.tensor_reduce(top[:].rearrange("p q h -> p (q h)"),
                                          mx[:, slot % 2, :].rearrange("p (q k) -> p q k", q=Q), AX.X,
                                          ALU.max).then_inc(top_own, 1)
                        dve.wait_ge(top_own, q + 1)
                    else:
                        for j in range(Q):
                            dve.wait_ge(mx_done, q * Q + (j + 1))
                            dve.tensor_reduce(top[:, j, :], mx[:, j, 0:H * P].rearrange("p (h k) -> p h k", h=H), AX.X,
                                              ALU.max).then_inc(top_own, 1)
                        dve.wait_ge(top_own, q * Q + Q)
                    for j in range(Q):
                        m = best[:, ds(b[j], 1), :]
                        dve.tensor_tensor(m, m, top[:, j, :].unsqueeze(1), ALU.max).then_inc(upd_own, 1)
                        dve.wait_ge(upd_own, q * Q + (j + 1))
                steps(dve, n, [(0, onehot)] * dot + [(1, score), (2, split), (3, exclude), (4, update)], lead=8,
                      unroll=G4)


def edge_sum(nc, core, L, name, acc, width, table=None, kept=None, heads=0, val=None, ma=None, slope=None,
             scale=1.0):
    H, W = heads, width
    HA = H * (2 if slope is not None else 1)
    R = W + H
    with Phase(nc, name) as ph:
        ix = ph.sb("ix", [P, G4, Q], I32)
        rows = ph.sb("rows", [P, G4, Q, W]) if kept is None else None
        s4 = ph.sb("s4", [P, 2, Q, P])
        o = ph.ps("o", [P, Q, 512])
        (ix_ready, taken, s_ready, out_done, acc_own, rows_used) = [ph.sem(n) for n in (
            "ix_ready", "taken", "s_ready", "out_done", "acc_own", "rows_used")]
        got = [ph.gathered_sem(k) for k in range(G4)]
        if H:
            st = ph.sb("st", [P, 2, Q, P])
            wr = ph.sb("weighted", [P, 2, Q, R])
            e = ph.sb("e", [P, 2, Q, HA])
            stp = ph.ps("stp", [P, Q, P])
            mep = ph.ps("mep", [P, 2, 512])
            st_turned, st_ready, me_done, e_own, ex_ready = [ph.sem(n) for n in (
                "st_turned", "st_ready", "me_done", "e_own", "ex_ready")]
            e_per = 5 if slope is not None else 1
        n = L.quads
        with nc.Block() as block:
            if kept is None:
                @block.gpsimd
                def _(pool):
                    bound = pool.to_reg(N - 1)

                    def gather(q, slot):
                        if H:
                            wait_free(pool, rows_used, q - (G4 - 1), q)
                        else:
                            wait_free(pool, out_done, (q - (G4 - 1)) * Q, q)
                        pool.wait_ge(ix_ready, q + 1)
                        pool.sem_inc(taken, 1)
                        gather_quad(pool, table, ix[:, slot], rows[:, slot], got[slot], bound)
                    steps(pool, n, [(0, gather)], unroll=G4, lead=8)

            @block.scalar
            def _(act):
                def index(q, slot):
                    wait_free(act, got[slot], (q - slot) * (16 * Q // G4), q)
                    act.copy(ix[:, slot, :], L.src[:, ds(q * Q, Q)]).then_inc(ix_ready, 1)

                def copy_st(q, slot):
                    act.wait_ge(st_turned, q + 1)
                    wait_free(act, me_done, q - 1, q)
                    act.copy(st[:, slot % 2], stp[:]).then_inc(st_ready, 1)

                def expo(q, slot):
                    act.wait_ge(e_own, (q + 1) * e_per)
                    wait_free(act, out_done, (q - 1) * Q, q)
                    act.activation(wr[:, slot % 2, :, W:R], e[:, slot % 2, :, 0:H], ACT.Exp,
                                   scale=scale).then_inc(ex_ready, 1)
                stages = [(0, index)] * (kept is None)
                if H:
                    stages += [(1, copy_st), (2, expo)]
                if stages:
                    steps(act, n, stages, unroll=G4, lead=8)

            @block.tensor
            def _(pe):
                def turn_s(q, slot):
                    pe.wait_ge(s_ready, (q + 1) * Q)
                    wait_free(pe, st_ready, q, q)
                    for j in range(Q):
                        ins = pe.transpose(stp[:, j, :], s4[:, slot % 2, j, :], core.ident[:])
                    ins.then_inc(st_turned, 1)

                def maxima(q, slot):
                    b = blocks_of(nc, mybir.EngineType.PE, L, q)
                    pe.wait_ge(st_ready, q + 1)
                    wait_free(pe, e_own, (q - 1) * e_per, q)
                    for j in range(Q):
                        ins = pe.matmul(mep[:, slot % 2, j * HA:(j + 1) * HA], st[:, slot % 2, j, :],
                                        ma[:, ds(b[j], 1), :].rearrange("p o d -> p (o d)"), start=True, stop=True)
                    ins.then_inc(me_done, 1)

                def collect(q, slot):
                    if H:
                        pe.wait_ge(rows_used, q + 1)
                    else:
                        pe.wait_ge(s_ready, (q + 1) * Q)
                        pe.wait_ge(got[slot], (q - slot) * (16 * Q // G4) + 16 * Q)
                    for j in range(Q):
                        wait_free(pe, acc_own, q * Q + (j - Q + 1), q)
                        rhs = wr[:, slot % 2, j, :] if H else rows[:, slot, j, :]
                        ins = pe.matmul(o[:, j, 0:R], s4[:, slot % 2, j, :], rhs, start=True, stop=True)
                        ins.then_inc(out_done, 1)
                if H:
                    steps(pe, n, [(0, turn_s), (1, maxima), (2, collect)], unroll=G4, lead=8)
                else:
                    steps(pe, n, [(1, collect)], unroll=G4, lead=8)

            @block.vector
            def _(dve):
                if H:
                    oe = Own(dve, e_own, e_per)

                def onehot(q, slot):
                    wait_free(dve, out_done, q * Q - Q, q)
                    for j in range(Q):
                        dve.tensor_scalar(s4[:, slot % 2, j, :], core.row[:], L.dst[:, ds(q * Q + j, 1)], None,
                                          ALU.is_equal).then_inc(s_ready, 1)

                def exponent(q, slot):
                    dve.wait_ge(me_done, q + 1)
                    wait_free(dve, ex_ready, q - 1, q)
                    oe.at(q)
                    eb, mb, v = e[:, slot % 2], mep[:, slot % 2, 0:Q * HA].rearrange("p (q h) -> p q h", q=Q), val[:, ds(q * Q, Q), :]
                    if slope is None:
                        oe.mark(dve.tensor_tensor(eb, v, mb, ALU.subtract))
                    else:
                        mx, sc = eb[:, :, 0:H], eb[:, :, H:]
                        oe.then(dve.tensor_copy(eb, mb))
                        oe.then(dve.tensor_tensor(mx, mx, sc, ALU.add))
                        oe.then(dve.tensor_tensor(sc, sc, v, ALU.add))
                        oe.then(dve.scalar_tensor_tensor(out=eb, in0=eb, scalar=slope, in1=eb,
                                                         op0=ALU.mult, op1=ALU.max))
                        oe.mark(dve.tensor_tensor(mx, sc, mx, ALU.subtract))

                def weigh(q, slot):
                    dve.wait_ge(ex_ready, q + 1)
                    if kept is None:
                        dve.wait_ge(got[slot], (q - slot) * (16 * Q // G4) + 16 * Q)
                        src = rows[:, slot]
                    else:
                        src = kept[:, ds(q * Q, Q), kept.shape[2] - W:]
                    r = wr[:, slot % 2]
                    c = W // H
                    by_head = lambda ap: ap.rearrange("p q (h c) -> p q h c", h=H)
                    dve.tensor_tensor(by_head(r[:, :, 0:W]), by_head(src), bc(r[:, :, W:R], 3, [P, Q, H, c]),
                                      ALU.mult).then_inc(rows_used, 1)

                def add(q, slot):
                    b = blocks_of(nc, mybir.EngineType.DVE, L, q)
                    for j in range(Q):
                        dve.wait_ge(out_done, q * Q + (j + 1))
                        wait_free(dve, acc_own, q * Q + j, q)
                        a = acc[:, ds(b[j], 1), :]
                        dve.tensor_tensor(a, a, o[:, j, 0:R].unsqueeze(1), ALU.add).then_inc(acc_own, 1)
                if H:
                    steps(dve, n, [(0, onehot), (1, exponent), (2, weigh), (3, add)], unroll=G4, lead=8)
                else:
                    steps(dve, n, [(0, onehot), (2, add)], unroll=G4, lead=8)


def finish_gnn(nc, core, name, acc, heads, table=None, select=False):
    W = D
    with Phase(nc, name) as ph:
        tb = ph.sb("tb", [P, 2, table.shape[1]]) if table is not None else None
        v = ph.sb("v", [P, 2, D])
        den = ph.sb("den", [P, T, 2 * heads]) if heads else None
        has = ph.sb("has", [P, T, 2]) if select else None
        got = [ph.sem("got0"), ph.sem("got1")]
        own, pre = ph.sem("own"), ph.sem("pre")
        per = 1 + 2 * (heads > 0) + 2 * select
        with nc.Block() as block:
            if table is not None:
                @block.sync
                def _(sp):
                    def load(t, par):
                        wait_free(sp, own, (t - 1) * per, t)
                        sp.dma_start(tb[:, par, :], rows_of(table, t)).then_inc(got[par], 16)
                    steps(sp, T, [(0, load)])

            @block.vector
            def _(dve):
                flat = lambda ap: ap.rearrange("p o d -> p (o d)")
                if heads:
                    o = Own(dve, pre, 8).at(0)
                    if select:
                        o.then(dve.tensor_scalar(has[:, :, 0:1], acc[:, :, W:W + 1], 0.0, None, ALU.is_gt))
                        o.then(dve.tensor_scalar(has[:, :, 1:2], has[:, :, 0:1], -1.0, 1.0, ALU.mult, ALU.add))
                    o.then(dve.tensor_scalar(den[:, :, 0:heads], acc[:, :, W:W + heads], 1e-30, None, ALU.max))
                    o.then(dve.reciprocal(den[:, :, heads:], den[:, :, 0:heads]))
                ot = Own(dve, own, per)

                def tile(t, par):
                    ot.at(t)
                    a = flat(acc[:, ds(t, 1), 0:W])
                    x = flat(core.x[:, ds(t, 1), :])
                    if heads:
                        c = W // heads
                        wait_free(dve, own, t * per - per, t)
                        ot.then(dve.tensor_tensor(v[:, par, :].rearrange("p (h c) -> p h c", h=heads),
                                                  a.rearrange("p (h c) -> p h c", h=heads),
                                                  bc(flat(den[:, ds(t, 1), heads:]), 2, [P, heads, c]), ALU.mult))
                        dve.wait_ge(got[par], (t - par) * 8 + 16)
                        own_part = tb[:, par, D:2 * D] if select else tb[:, par, 0:D]
                        ot.then(dve.tensor_tensor(v[:, par, :], v[:, par, :], own_part, ALU.add))
                        a = v[:, par, :]
                        if select:
                            ot.then(dve.tensor_scalar(a, a, flat(has[:, ds(t, 1), 0:1]), None, ALU.mult))
                            ot.then(dve.scalar_tensor_tensor(out=a, in0=tb[:, par, 0:D],
                                                             scalar=flat(has[:, ds(t, 1), 1:2]), in1=a,
                                                             op0=ALU.mult, op1=ALU.add))
                    ot.mark(dve.scalar_tensor_tensor(out=x, in0=a, scalar=0.0, in1=x, op0=ALU.max, op1=ALU.add))
                steps(dve, T, [(0, tile)])



class Core:

    def __init__(self, nc, ctx):
        sb = lambda n, s, dt=F32: ctx.enter_context(nc.sbuf_tensor(n, s, dt))
        self.x = sb("x_all", [P, T, D])
        self.ident = sb("ident", [P, P])
        self.tri = sb("tri", [P, P])
        self.ones = sb("ones", [P, P])
        self.row = sb("row", [P, P])
        self.part = sb("part", [P, 1])
        self.ident_b = sb("ident_b", [P, P], BF16)
        self.ident4_b = sb("ident4_b", [P, 4, P], BF16)
        Phase.gathered = [ctx.enter_context(nc.semaphore(f"gathered{k}")) for k in range(4)]
        self.rstd = sb("rstd", [P, T])
        self.nmean = sb("nmean", [P, T])


def load_x(nc, core, x):
    with Phase(nc, "load_x") as ph:
        zeroed, got = ph.sem("zeroed"), ph.sem("got")
        with nc.Block() as block:
            @block.vector
            def _(dve):
                dve.memset(core.x[:, T - 1, :], 0.0).then_inc(zeroed, 1)

            @block.sync
            def _(sp):
                sp.dma_start(core.x[:, 0:T - 1, :], x[0:(T - 1) * P, :].rearrange("(t p) d -> p t d", p=P)).then_inc(got, 16)
                sp.wait_ge(zeroed, 1)
                sp.dma_start(core.x[0:LAST, T - 1, :], x[(T - 1) * P:N, :]).then_inc(got, 16)
                sp.wait_ge(got, 32)


def store_x(nc, core, out):
    with Phase(nc, "store_x") as ph:
        stored = ph.sem("stored")
        with nc.Block() as block:
            @block.sync
            def _(sp):
                sp.dma_start(out[0:(T - 1) * P, :].rearrange("(t p) d -> p t d", p=P), core.x[:, 0:T - 1, :]).then_inc(stored, 16)
                sp.dma_start(out[(T - 1) * P:N, :], core.x[0:LAST, T - 1, :]).then_inc(stored, 16)
                sp.wait_ge(stored, 32)


def fill(nc, name, items):
    with Phase(nc, name) as ph:
        with nc.Block() as block:
            @block.vector
            def _(dve):
                for ap, v in items:
                    dve.memset(ap, v)


def layer0_gnn(nc, core, main, w):
    keys = nc.dram_tensor("keys", [T * P, D], F32).ap()
    values = nc.dram_tensor("values", [T * P, D], F32).ap()
    skip = nc.dram_tensor("skip", [T * P, D], F32).ap()
    with ExitStack() as ctx:
        sb = lambda n, s, dt=F32: ctx.enter_context(nc.sbuf_tensor(n, s, dt))
        best = sb("l0_best", [P, T, 4])
        score = sb("l0_score", [P, main.tiles, 4])
        acc = sb("l0_acc", [P, T, D + 4])
        queries = acc[:, :, 0:D]
        with nc.sbuf_tensor("l0_z", [P, T, D], F32) as z:
            statistics(nc, core, core.x, "l0_stat_a")
            normalize(nc, core, z, "l0_norm")
            statistics(nc, core, z, "l0_stat_b")
            project(nc, core, "l0_proj", z, 4 * D,
                    [(0, w["Wq"]), (D, w["Wk"]), (2 * D, w["Wv"]), (3 * D, w["Wskip"])],
                    bias_loads=[(0, w["bq"]), (D, w["bk"]), (2 * D, w["bv"]), (3 * D, w["bskip"])],
                    affine=(w["ln_gamma"], w["ln_beta"]),
                    stores=[(keys, "out", D, 2 * D, 0), (values, "out", 2 * D, 3 * D, 0),
                            (skip, "out", 3 * D, 4 * D, 0)],
                    to_sbuf=[(queries, 0)])
        fill(nc, "l0_fill", [(best[:], -FAR)])
        edge_max(nc, core, main, "l0_max", 4, keys, D, score, best, queries=queries)
        fill(nc, "l0_fill_acc", [(acc[:], 0.0)])
        edge_sum(nc, core, main, "l0_sum", acc, D, table=values, heads=4, val=score, ma=best, scale=0.125)
        finish_gnn(nc, core, "l0_finish", acc, 4, table=skip)


S2 = 2 * P


class Routing:

    def __init__(self, nc, ctx, name, experts, k):
        self.E, self.K, self.name = experts, k, name
        self.runs = (k * N + experts * (S2 - 1)) // S2
        self.runs += self.runs % 2
        sb = lambda n, s, dt=F32: ctx.enter_context(nc.sbuf_tensor(f"{name}_{n}", s, dt))
        self.weight = sb("weight", [P, T, k])
        self.put = sb("put", [P, T, k], I32)
        self.take = sb("take", [P, T, k], I32)
        self.expert = sb("expert", [1, self.runs], I32)


def route(nc, core, R, logits, mode, capacity=None):
    E, K, runs = R.E, R.K, R.runs
    with Phase(nc, f"{R.name}_route") as ph:
        s = ph.sb("s", [P, T, E])
        tmp = ph.sb("tmp", [P, T, E])
        oh = ph.sb("oh", [P, K, T, E])
        both = ph.sb("both", [P, T, E])
        rank = ph.sb("rank", [P, T, E])
        tot = ph.sb("tot", [P, E, T])
        run_tot = ph.sb("run_tot", [P, E, T])
        keep = ph.sb("keep", [P, E, T])
        m = ph.sb("m", [P, K, T])
        first = ph.sb("first", [P, T])
        valid = ph.sb("valid", [P, T])
        diff = ph.sb("diff", [P, T])
        w = ph.sb("w", [P, K, T])
        pos = ph.sb("pos", [P, T])
        late = ph.sb("late", [P, T])
        nt = ph.sb("nt", [P, E])
        nti = ph.sb("nti", [P, E], I32)
        ends = ph.sb("ends", [P, E])
        ones_e = ph.sb("ones_e", [P, E])
        run_i = ph.sb("run_i", [1, runs], I32)
        run_f = ph.sb("run_f", [1, runs])
        cmp = ph.sb("cmp", [1, runs, E])
        pre = ph.ps("pre", [P, T * E])
        totp = ph.ps("totp", [P, T * E])
        own, exp_in, exp_out, ranked, counted, numbered = [ph.sem(n) for n in (
            "own", "exp_in", "exp_out", "ranked", "counted", "numbered")]
        flat = lambda ap: ap.rearrange("p a b -> p (a b)")
        with nc.Block() as block:
            @block.gpsimd
            def _(pool):
                pool.iota(run_i[:], pattern=[[1, runs]], base=0, channel_multiplier=0).then_inc(numbered, 1)

            @block.scalar
            def _(act):
                if mode == "all":
                    act.wait_ge(exp_in, 1)
                    act.activation(flat(s[:]), flat(s[:]), ACT.Exp).then_inc(exp_out, 1)
                else:
                    act.wait_ge(exp_in, 1)
                    act.activation(diff[:], diff[:], ACT.Exp).then_inc(exp_out, 1)

            @block.tensor
            def _(pe):
                pe.wait_ge(ranked, 1)
                pe.matmul(pre[:], core.tri[:], flat(both[:]), start=True, stop=True)
                pe.matmul(totp[:], core.ones[:], flat(both[:]), start=True, stop=True).then_inc(counted, 1)

            @block.vector
            def _(dve):
                o = Own(dve, own, 200).at(0)
                over_e = lambda ap: bc(ap, 2, [P, T, E])
                names = bc(core.row[:, 0:E], 1, [P, T, E])
                if mode == "all":
                    o.then(dve.tensor_reduce(first[:], logits[:, :, 0:E], AX.X, ALU.max))
                    dve.tensor_tensor(s[:], logits[:, :, 0:E], over_e(first[:]), ALU.subtract).then_inc(exp_in, 1)
                    dve.wait_ge(exp_out, 1)
                    o.then(dve.tensor_reduce(first[:], s[:], AX.X, ALU.add))
                    o.then(dve.reciprocal(first[:], first[:]))
                    o.then(dve.tensor_tensor(s[:], s[:], over_e(first[:]), ALU.mult))
                else:
                    o.then(dve.tensor_copy(s[:], logits[:, :, 0:E]))
                o.then(dve.memset(valid[:], 1.0))
                o.then(dve.tensor_scalar(valid[:, T - 1:T], core.part[:], float(LAST), None, ALU.is_lt))
                for k in range(K):
                    o.then(dve.tensor_reduce(m[:, k, :], s[:], AX.X, ALU.max))
                    o.then(dve.tensor_tensor(tmp[:], s[:], over_e(m[:, k, :]), ALU.not_equal))
                    o.then(dve.scalar_tensor_tensor(out=tmp[:], in0=tmp[:], scalar=float(P), in1=names,
                                                    op0=ALU.mult, op1=ALU.add))
                    o.then(dve.tensor_reduce(first[:], tmp[:], AX.X, ALU.min))
                    o.then(dve.tensor_tensor(oh[:, k], names, over_e(first[:]), ALU.is_equal))
                    if k + 1 < K:
                        o.then(dve.tensor_scalar(tmp[:], oh[:, k], -1.0, 1.0, ALU.mult, ALU.add))
                        o.then(dve.tensor_tensor(s[:], s[:], tmp[:], ALU.mult))
                        o.then(dve.scalar_tensor_tensor(out=s[:], in0=oh[:, k], scalar=-FAR, in1=s[:],
                                                        op0=ALU.mult, op1=ALU.add))
                    o.then(dve.tensor_tensor(oh[:, k], oh[:, k], over_e(valid[:]), ALU.mult))
                if K == 2:
                    dve.tensor_tensor(both[:], oh[:, 0], oh[:, 1], ALU.add).then_inc(ranked, 1)
                else:
                    dve.tensor_copy(both[:], oh[:, 0]).then_inc(ranked, 1)
                if mode == "top":
                    dve.tensor_tensor(diff[:], m[:, 1, :], m[:, 0, :], ALU.subtract).then_inc(exp_in, 1)
                    dve.wait_ge(exp_out, 1)
                    o.then(dve.tensor_scalar(first[:], diff[:], 1.0, None, ALU.add))
                    o.then(dve.reciprocal(w[:, 0, :], first[:]))
                    o.then(dve.tensor_tensor(w[:, 1, :], diff[:], w[:, 0, :], ALU.mult))
                elif K == 2:
                    o.then(dve.tensor_tensor(first[:], m[:, 0, :], m[:, 1, :], ALU.add))
                    o.then(dve.tensor_scalar(first[:], first[:], 1e-12, None, ALU.max))
                    o.then(dve.reciprocal(first[:], first[:]))
                    for k in range(K):
                        o.then(dve.tensor_tensor(w[:, k, :], m[:, k, :], first[:], ALU.mult))
                else:
                    o.then(dve.tensor_copy(w[:, 0, :], m[:, 0, :]))
                dve.wait_ge(counted, 1)
                o.then(dve.tensor_copy(tot[:], totp[:].rearrange("p (t e) -> p e t", e=E)))
                o.then(dve.memset(keep[:], 1.0))
                o.then(dve.memset(keep[:, :, 0:1], 0.0))
                o.then(dve.tensor_tensor_scan(flat(run_tot[:]), flat(keep[:]), flat(tot[:]), 0.0, ALU.mult, ALU.add))
                o.then(dve.tensor_scalar(nt[:], run_tot[:, :, T - 1], S2 - 1.0, None, ALU.add))
                o.then(dve.tensor_tensor(tot[:], run_tot[:], tot[:], ALU.subtract))
                o.then(dve.tensor_tensor(rank[:], pre[:].rearrange("p (t e) -> p t e", e=E),
                                         tot[:].rearrange("p e t -> p t e"), ALU.add))
                o.then(dve.tensor_copy(nti[:], nt[:]))
                o.then(dve.tensor_scalar(nti[:], nti[:], 8, None, ALU.logical_shift_right))
                o.then(dve.tensor_copy(nt[:], nti[:]))
                o.then(dve.memset(ones_e[:], 1.0))
                o.then(dve.tensor_tensor_scan(ends[:], ones_e[:], nt[:], 0.0, ALU.mult, ALU.add))
                o.then(dve.tensor_tensor(nt[:], ends[:], nt[:], ALU.subtract))
                o.then(dve.tensor_scalar(nt[:], nt[:], float(S2), None, ALU.mult))
                if capacity is not None:
                    o.then(dve.tensor_tensor(tmp[:], oh[:, 0], rank[:], ALU.mult))
                    o.then(dve.tensor_reduce(pos[:], tmp[:], AX.X, ALU.add))
                    o.then(dve.tensor_scalar(pos[:], pos[:], float(capacity), None, ALU.is_lt))
                    o.then(dve.tensor_tensor(w[:, 0, :], w[:, 0, :], pos[:], ALU.mult))
                o.then(dve.tensor_tensor(rank[:], rank[:], bc(nt[:], 1, [P, T, E]), ALU.add))
                o.then(dve.tensor_scalar(late[:], valid[:], -1.0e7, 1.0e7, ALU.mult, ALU.add))
                for k in range(K):
                    o.then(dve.tensor_tensor(tmp[:], oh[:, k], rank[:], ALU.mult))
                    o.then(dve.tensor_reduce(pos[:], tmp[:], AX.X, ALU.add))
                    o.then(dve.tensor_copy(R.take[:, :, k], pos[:]))
                    o.then(dve.tensor_tensor(pos[:], pos[:], late[:], ALU.add))
                    o.then(dve.tensor_copy(R.put[:, :, k], pos[:]))
                    o.then(dve.tensor_tensor(R.weight[:, :, k], w[:, k, :], valid[:], ALU.mult))
                dve.wait_ge(numbered, 1)
                o.then(dve.tensor_copy(run_f[:], run_i[:]))
                o.then(dve.tensor_tensor(cmp[:], bc(run_f[:], 2, [1, runs, E]), bc(ends[0:1, :], 1, [1, runs, E]),
                                         ALU.is_ge))
                o.then(dve.tensor_reduce(run_f[:], cmp[:], AX.X, ALU.add))
                o.then(dve.tensor_scalar(run_f[:], run_f[:], E - 1.0, None, ALU.min))
                o.then(dve.tensor_copy(R.expert[:], run_f[:]))


def dispatch(nc, core, R, z, sorted_rows):
    K, total = R.K, R.runs * S2
    with Phase(nc, f"{R.name}_put") as ph:
        zero = ph.sb("zero", [P, 2 * D])
        rows = ph.sb("rows", [P, G4, D])
        ix = ph.sb("ix", [P, G4, K], I32)
        zeroed, cleared, staged, taken = [ph.sem(n) for n in ("zeroed", "cleared", "staged", "taken")]
        put = [ph.gathered_sem(k) for k in range(G4)]
        with nc.Block() as block:
            @block.vector
            def _(dve):
                dve.memset(zero[:], 0.0).then_inc(zeroed, 1)

            @block.sync
            def _(sp):
                sp.wait_ge(zeroed, 1)
                sp.dma_start(sorted_rows.rearrange("(p r k) d -> p r (k d)", p=P, k=2),
                             bc(zero[:], 1, [P, R.runs, 2 * D])).then_inc(cleared, 16)
                for g in range(G4):
                    sp.wait_ge(put[g], 16 * K * len(range(g, T, G4)))

            @block.scalar
            def _(act):
                def stage(t, slot):
                    wait_free(act, put[slot], (t - slot) * (16 * K // G4), t)
                    act.copy(ix[:, slot, :], R.put[:, ds(t, 1), :].rearrange("p o k -> p (o k)"))
                    act.copy(rows[:, slot, :], z[:, ds(t, 1), :].rearrange("p o d -> p (o d)")).then_inc(staged, 1)
                steps(act, T, [(0, stage)], unroll=G4)

            @block.gpsimd
            def _(pool):
                pool.wait_ge(cleared, 16)
                bound = pool.to_reg(total - 1)

                def scatter(t, slot):
                    pool.wait_ge(staged, t + 1)
                    pool.sem_inc(taken, 1)
                    for k in range(K):
                        pool.indirect_dma_start(sorted_rows,
                                                bass.IndirectOffsetOnAxis(ap=ix[:, slot, k:k + 1], axis=0),
                                                rows[:, slot, :], None, bounds_check=bound,
                                                oob_is_err=False).then_inc(put[slot], 16)
                steps(pool, T, [(0, scatter)], unroll=G4)


def experts(nc, core, R, sorted_rows, results, w1, b1, w2, b2, act_fn):
    E, _, HID = w1.shape
    HC = HID // P
    runs = R.runs
    with Phase(nc, f"{R.name}_ffn") as ph:
        xs = ph.sb("xs", [P, 2, 2, D])
        xt = ph.sb("xt", [P, 2, DC, S2])
        w1b = ph.sb("w1b", [P, 2, DC, HID])
        w2b = ph.sb("w2b", [P, 2, HC, D])
        b2b = ph.sb("b2b", [P, 2, D])
        b1r = ph.sb("b1r", [E * HC, P])
        b1t = ph.sb("b1t", [P, E * HC])
        ht = ph.sb("ht", [P, 2, HC, S2])
        ys = ph.sb("ys", [P, 2, 2, D])
        xtp = ph.ps("xtp", [P, 2, DC, S2])
        hp = ph.ps("hp", [P, 4, 512])
        yp = ph.ps("yp", [P, 2, 2, D])
        stored_seen = ph.sem("stored_seen")
        b_in, b_turned, b_ready, turned, xt_ready, h_done, ht_ready, y_done, y_ready = [ph.sem(n) for n in (
            "b_in", "b_turned", "b_ready", "turned", "xt_ready", "h_done", "ht_ready", "y_done", "y_ready")]
        x_in, w1_in, w2_in = [[ph.sem(f"{n}{k}") for k in range(2)] for n in ("x_in", "w1_in", "w2_in")]
        y_out = [ph.gathered_sem(k) for k in range(2)]
        with nc.Block() as block:
            @block.sync
            def _(sp):
                sp.dma_start(b1r[:], b1.rearrange("e (c p) -> (e c) p", p=P)).then_inc(b_in, 16)

                def load(q, par):
                    sp_e = nc.values_load(R.expert[0:1, ds(q, 1)], engines=(mybir.EngineType.SP,), min_val=0,
                                          max_val=E - 1, skip_runtime_bounds_check_because="made below E on chip")
                    wait_free(sp, turned, q - 1, q)
                    sp.dma_start(xs[:, par], sorted_rows[ds(q * S2, S2), :].rearrange("(h p) d -> p h d", p=P)
                                 ).then_inc(x_in[par], 16)
                    wait_free(sp, h_done, (q - 1) * HC, q)
                    sp.dma_start(w1b[:, par], w1[ds(sp_e, 1), :, :].rearrange("o (c p) h -> p (o c) h", p=P)
                                 ).then_inc(w1_in[par], 16)
                    wait_free(sp, y_done, q - 1, q)
                    sp.dma_start(w2b[:, par], w2[ds(sp_e, 1), :, :].rearrange("o (c p) d -> p (o c) d", p=P)
                                 ).then_inc(w2_in[par], 16)
                    wait_free(sp, y_ready, q - 1, q)
                    sp.dma_start(b2b[:, par, :], b2[ds(sp_e, 1), :].to_broadcast([P, D])).then_inc(w2_in[par], 16)
                steps(sp, runs, [(0, load)])

            @block.gpsimd
            def _(pool):
                def store(q, par):
                    pool.wait_ge(y_ready, q + 1)
                    pool.sem_inc(stored_seen, 1)
                    pool.dma_start(results[ds(q * S2, S2), :].rearrange("(h p) d -> p h d", p=P),
                                   ys[:, par]).then_inc(y_out[par], 16)
                steps(pool, runs, [(0, store)])
                pool.wait_ge(y_out[0], 8 * runs)
                pool.wait_ge(y_out[1], 8 * runs)

            @block.tensor
            def _(pe):
                pe.wait_ge(b_in, 16)
                pe.transpose(hp[:, 0, 0:E * HC], b1r[:], core.ident[0:E * HC, 0:E * HC]).then_inc(b_turned, 1)
                pe.wait_ge(b_ready, 1)

                def turn(q, par):
                    pe.wait_ge(x_in[par], (q - par) * 8 + 16)
                    wait_free(pe, xt_ready, q - 1, q)
                    for h in range(2):
                        for c in range(DC):
                            ins = pe.transpose(xtp[:, par, c, h * P:(h + 1) * P], xs[:, par, h, c * P:(c + 1) * P],
                                               core.ident[:])
                    ins.then_inc(turned, 1)

                def up(q, par):
                    pe.wait_ge(xt_ready, q + 1)
                    pe.wait_ge(w1_in[par], (q - par) * 8 + 16)
                    for k in range(HC):
                        if k < 4:
                            wait_free(pe, ht_ready, q * HC + (k - 3), q)
                        else:
                            pe.wait_ge(ht_ready, q * HC + (k - 3))
                        for c in range(DC):
                            ins = pe.matmul(hp[:, k % 4, 0:S2], w1b[:, par, c, k * P:(k + 1) * P], xt[:, par, c, :],
                                            start=(c == 0), stop=(c == DC - 1))
                        ins.then_inc(h_done, 1)

                def down(q, par):
                    pe.wait_ge(ht_ready, (q + 1) * HC)
                    pe.wait_ge(w2_in[par], (q - par) * 16 + 32)
                    wait_free(pe, y_ready, q - 1, q)
                    for h in range(2):
                        for k in range(HC):
                            ins = pe.matmul(yp[:, par, h, :], ht[:, par, k, h * P:(h + 1) * P], w2b[:, par, k, :],
                                            start=(k == 0), stop=(k == HC - 1))
                    ins.then_inc(y_done, 1)
                steps(pe, runs, [(0, turn), (1, up), (2, down)])

            @block.scalar
            def _(act):
                act.wait_ge(b_turned, 1)
                act.copy(b1t[:], hp[:, 0, 0:E * HC]).then_inc(b_ready, 1)
                act.wait_ge(b_ready, 1)

                def activate(q, par):
                    e = nc.values_load(R.expert[0:1, ds(q, 1)], engines=(mybir.EngineType.Activation,), min_val=0,
                                       max_val=E - 1, skip_runtime_bounds_check_because="made below E on chip")
                    wait_free(act, y_done, q - 1, q)
                    for k in range(HC):
                        act.wait_ge(h_done, q * HC + (k + 1))
                        act.activation(ht[:, par, k, :], hp[:, k % 4, 0:S2], act_fn,
                                       bias=b1t[:, ds(e * HC + k, 1)]).then_inc(ht_ready, 1)
                steps(act, runs, [(1, activate)])

            @block.vector
            def _(dve):
                def copy_x(q, par):
                    dve.wait_ge(turned, q + 1)
                    wait_free(dve, h_done, (q - 1) * HC, q)
                    dve.tensor_copy(xt[:, par], xtp[:, par]).then_inc(xt_ready, 1)

                def finish(q, par):
                    dve.wait_ge(y_done, q + 1)
                    wait_free(dve, y_out[par], (q - par) * 8, q)
                    dve.tensor_tensor(ys[:, par], yp[:, par], bc(b2b[:, par, :], 1, [P, 2, D]),
                                      ALU.add).then_inc(y_ready, 1)
                steps(dve, runs, [(0, copy_x), (2, finish)])


def combine(nc, core, R, results, products=None):
    K, total = R.K, R.runs * S2
    CH = 7
    assert T % CH == 0
    with Phase(nc, f"{R.name}_take") as ph:
        rows = ph.sb("rows", [P, G4, K, D])
        ix = ph.sb("ix", [P, G4, K], I32)
        if products is not None:
            bad = ph.sb("bad", [P, CH * D], U32)
            subst = ph.sb("subst", [P, 3, CH * D])
        staged, taken, own, consts, clean = [ph.sem(n) for n in ("staged", "taken", "own", "consts", "clean")]
        got = [ph.gathered_sem(k) for k in range(G4)]
        with nc.Block() as block:
            @block.scalar
            def _(act):
                def stage(t, slot):
                    wait_free(act, got[slot], (t - slot) * (16 * K // G4), t)
                    act.copy(ix[:, slot, :], R.take[:, ds(t, 1), :].rearrange("p o k -> p (o k)")).then_inc(staged, 1)
                steps(act, T, [(0, stage)], unroll=G4)

            @block.gpsimd
            def _(pool):
                bound = pool.to_reg(total - 1)

                def gather(t, slot):
                    wait_free(pool, own, (t - 3) * K, t)
                    pool.wait_ge(staged, t + 1)
                    pool.sem_inc(taken, 1)
                    for k in range(K):
                        pool.indirect_dma_start(rows[:, slot, k, :], None, results,
                                                bass.IndirectOffsetOnAxis(ap=ix[:, slot, k:k + 1], axis=0),
                                                bounds_check=bound, oob_is_err=False).then_inc(got[slot], 16)
                steps(pool, T, [(0, gather)], unroll=G4)

            @block.vector
            def _(dve):
                o = Own(dve, own, K)

                def add(t, slot):
                    dve.wait_ge(got[slot], (t - slot) * (16 * K // G4) + 16 * K)
                    o.at(t)
                    x = core.x[:, ds(t, 1), :].rearrange("p o d -> p (o d)")
                    for k in range(K):
                        weight = R.weight[:, ds(t, 1), k:k + 1].rearrange("p o k -> p (o k)")
                        if products is None:
                            o.then(dve.scalar_tensor_tensor(out=x, in0=rows[:, slot, k, :], scalar=weight, in1=x,
                                                            op0=ALU.mult, op1=ALU.add))
                        else:
                            o.mark(dve.tensor_scalar(products[:, ds(t, 1), :].rearrange("p o d -> p (o d)"),
                                                     rows[:, slot, k, :], weight, None, ALU.mult))
                steps(dve, T, [(0, add)], unroll=G4)
                if products is None:
                    return
                for k, value in enumerate((0.0, 1.0e4, -1.0e4)):
                    dve.memset(subst[:, k, :], value).then_inc(consts, 1)
                dve.wait_ge(consts, 3)
                dve.wait_ge(own, T * K)
                largest = 3.4028234663852886e38
                c = Own(dve, clean, 7 * (T // CH)).at(0)
                for t in range(0, T, CH):
                    v = products[:, t:t + CH, :].rearrange("p t d -> p (t d)")
                    c.then(dve.tensor_tensor(bad[:], v, v, ALU.not_equal))
                    c.then(dve.copy_predicated(v, bad[:], subst[:, 0, :]))
                    c.then(dve.tensor_scalar(bad[:], v, largest, None, ALU.is_gt))
                    c.then(dve.copy_predicated(v, bad[:], subst[:, 1, :]))
                    c.then(dve.tensor_scalar(bad[:], v, -largest, None, ALU.is_lt))
                    c.then(dve.copy_predicated(v, bad[:], subst[:, 2, :]))
                    x = core.x[:, t:t + CH, :].rearrange("p t d -> p (t d)")
                    c.mark(dve.tensor_tensor(x, x, v, ALU.add))


def mixture(nc, core, name, logits, mode, k, z, w1, b1, w2, b2, act_fn, capacity=None):
    with ExitStack() as ctx:
        R = Routing(nc, ctx, name, w1.shape[0], k)
        sorted_rows = nc.dram_tensor(f"{name}_rows", [R.runs * S2, D], F32).ap()
        results = nc.dram_tensor(f"{name}_results", [R.runs * S2, D], F32).ap()
        route(nc, core, R, logits, mode, capacity)
        dispatch(nc, core, R, z, sorted_rows)
        experts(nc, core, R, sorted_rows, results, w1, b1, w2, b2, act_fn)
        combine(nc, core, R, results, products=z if capacity is not None else None)


def layer0_ffn(nc, core, w):
    with ExitStack() as ctx:
        sb = lambda n, s, dt=F32: ctx.enter_context(nc.sbuf_tensor(n, s, dt))
        z = sb("m0_z", [P, T, D])
        logits = sb("m0_logits", [P, T, 8])
        statistics(nc, core, core.x, "m0_stat_a")
        normalize(nc, core, z, "m0_norm", add=False)
        statistics(nc, core, z, "m0_stat_b")
        project(nc, core, "m0_proj", z, 8, [(0, w["Wr"])], bias_loads=[(0, w["br"])],
                affine=(w["gamma"], w["beta"]), keep_z=z, to_sbuf=[(logits, 0)])
        mixture(nc, core, "m0", logits, "top", 2, z, w["W1"], w["b1"], w["W2"], w["b2"], ACT.Gelu)


def layer1_gnn(nc, core, back, w):
    feats = nc.dram_tensor("l1_feats", [T * P, D], F32).ap()
    with nc.sbuf_tensor("l1_acc", [P, T, D], F32) as acc:
        statistics(nc, core, core.x, "l1_stat")
        project(nc, core, "l1_proj", core.x, 2 * D, [(0, w["w0"]), (D, w["w1"])],
                stores=[(feats, "out", D, 2 * D, 0)], to_sbuf=[(acc, 0)])
        edge_sum(nc, core, back, "l1_sum", acc, D, table=feats)
        finish_gnn(nc, core, "l1_finish", acc, 0)


def layer2_ffn(nc, core, w):
    with ExitStack() as ctx:
        sb = lambda n, s, dt=F32: ctx.enter_context(nc.sbuf_tensor(n, s, dt))
        z = sb("m2_z", [P, T, D])
        logits = sb("m2_logits", [P, T, 8])
        wr = sb("m2_router", [P, DC, 8])
        load_transposed(nc, core, [(wr, w["router_w"])], "m2_turn")
        statistics(nc, core, core.x, "m2_stat")
        project(nc, core, "m2_proj", core.x, 8, [], w_sb=wr, add_to_x=True, keep_z=z, to_sbuf=[(logits, 0)])
        mixture(nc, core, "m2", logits, "all", 2, z, w["w1"], w["b1"], w["w2"], w["b2"], ACT.Gelu)


def layer3_ffn(nc, core, w):
    E = w["w1"].shape[0]
    capacity = max(1, -(-5 * N // (4 * E)))
    with ExitStack() as ctx:
        sb = lambda n, s, dt=F32: ctx.enter_context(nc.sbuf_tensor(n, s, dt))
        z = sb("m3_z", [P, T, D])
        logits = sb("m3_logits", [P, T, 8])
        statistics(nc, core, core.x, "m3_stat")
        project(nc, core, "m3_proj", core.x, 8, [(0, w["gate_w"])], bias_loads=[(0, w["gate_b"])], keep_z=z,
                to_sbuf=[(logits, 0)])
        mixture(nc, core, "m3", logits, "all", 1, z, w["w1"], w["b1"], w["w2"], w["b2"], ACT.Relu, capacity=capacity)


def gat_self(nc, core, acc, ma, own_rows):
    H, C = 4, 4
    with Phase(nc, "gat_self") as ph:
        e = ph.sb("e", [P, T, 2 * H])
        ex = ph.sb("ex", [P, T, H])
        own, ready, done = ph.sem("own"), ph.sem("ready"), ph.sem("done")
        flat = lambda ap: ap.rearrange("p a b -> p (a b)")
        with nc.Block() as block:
            @block.vector
            def _(dve):
                o = Own(dve, own, 8).at(0)
                o.mark(dve.tensor_tensor(e[:, :, 0:H], own_rows[:, :, 0:H], ma[:, :, H:], ALU.add))
                o.then(dve.tensor_tensor(e[:, :, H:], ma[:, :, 0:H], ma[:, :, H:], ALU.add))
                o.then(dve.scalar_tensor_tensor(out=e[:], in0=e[:], scalar=0.2, in1=e[:], op0=ALU.mult, op1=ALU.max))
                dve.tensor_tensor(ex[:], e[:, :, 0:H], e[:, :, H:], ALU.subtract).then_inc(ready, 1)
                dve.wait_ge(done, 1)
                for h in range(H):
                    dve.tensor_tensor(acc[:, :, h * C:(h + 1) * C], own_rows[:, :, H + h * C:H + (h + 1) * C],
                                      ex[:, :, h:h + 1].to_broadcast([P, T, C]), ALU.mult)
                dve.tensor_copy(acc[:, :, H * C:], ex[:])

            @block.scalar
            def _(act):
                act.wait_ge(ready, 1)
                act.activation(flat(ex[:]), flat(ex[:]), ACT.Exp).then_inc(done, 1)


def gat_scores(nc, core, acc, scores, w):
    H, C = 4, 4
    F = H * C
    with Phase(nc, "gat_scores") as ph:
        v = ph.sb("v", [P, T, F])
        sq = ph.sb("sq", [P, T, F])
        den = ph.sb("den", [P, T, H])
        mean = ph.sb("mean", [P, T])
        var = ph.sb("var", [P, T])
        root = ph.sb("root", [P, T])
        r = ph.sb("r", [P, T])
        cst = ph.sb("cst", [P, 3, F])
        own, loaded, rooted = ph.sem("own"), ph.sem("loaded"), ph.sem("rooted")
        with nc.Block() as block:
            @block.sync
            def _(sp):
                for k, a in enumerate((w["b_gat"], w["ln_gamma"], w["ln_beta"])):
                    sp.dma_start(cst[:, k, :], a.rearrange("(o n) -> o n", o=1).to_broadcast([P, F])
                                 ).then_inc(loaded, 16)

            @block.vector
            def _(dve):
                o = Own(dve, own, 64).at(0)
                const = lambda k: bc(cst[:, k, :], 1, [P, T, F])
                over = lambda ap: bc(ap, 2, [P, T, F])
                o.then(dve.tensor_scalar(den[:], acc[:, :, F:], 1e-16, None, ALU.add))
                o.then(dve.reciprocal(den[:], den[:]))
                for h in range(H):
                    o.then(dve.tensor_tensor(v[:, :, h * C:(h + 1) * C], acc[:, :, h * C:(h + 1) * C],
                                             den[:, :, h:h + 1].to_broadcast([P, T, C]), ALU.mult))
                dve.wait_ge(loaded, 48)
                o.then(dve.tensor_tensor(v[:], v[:], const(0), ALU.add))
                o.then(dve.tensor_reduce(mean[:], v[:], AX.X, ALU.add))
                o.then(dve.tensor_scalar(mean[:], mean[:], 1.0 / F, None, ALU.mult))
                o.then(dve.tensor_tensor(v[:], v[:], over(mean[:]), ALU.subtract))
                o.then(dve.tensor_tensor(sq[:], v[:], v[:], ALU.mult))
                o.then(dve.tensor_reduce(var[:], sq[:], AX.X, ALU.add))
                o.then(dve.tensor_scalar(var[:], var[:], 1.0 / F, EPS, ALU.mult, ALU.add))
                before_root = o.k
                ph.before_root = before_root
                dve.wait_ge(rooted, 1)
                o.then(dve.reciprocal(r[:], root[:]))
                o.then(dve.tensor_tensor(mean[:], r[:], r[:], ALU.mult))
                o.then(dve.tensor_tensor(mean[:], mean[:], var[:], ALU.mult))
                o.then(dve.tensor_scalar(mean[:], mean[:], -0.5, 1.5, ALU.mult, ALU.add))
                o.then(dve.tensor_tensor(r[:], r[:], mean[:], ALU.mult))
                o.then(dve.tensor_tensor(v[:], v[:], over(r[:]), ALU.mult))
                o.then(dve.tensor_tensor(v[:], v[:], const(1), ALU.mult))
                o.then(dve.tensor_tensor(v[:], v[:], const(2), ALU.add))
                o.then(dve.tensor_reduce(scores[:], v[:].rearrange("p t (h e) -> p t e h", h=H), AX.X, ALU.add))
                o.then(dve.tensor_scalar(scores[:], scores[:], 1.0 / H, None, ALU.mult))

            @block.scalar
            def _(act):
                act.wait_ge(own, 13)
                act.activation(root[:], var[:], ACT.Sqrt).then_inc(rooted, 1)


def layer1_ffn(nc, core, gat, w):
    HE = 16
    table = nc.dram_tensor("gat_table", [T * P, 4 + HE], F32).ap()
    with ExitStack() as ctx:
        sb = lambda n, s, dt=F32: ctx.enter_context(nc.sbuf_tensor(n, s, dt))
        scores = sb("gat_score4", [P, T, 4])
        a_src = sb("gat_asrc", [P, T, 4])
        ma = sb("gat_ma", [P, T, 8])
        acc = sb("gat_acc", [P, T, HE + 4])
        own_rows = sb("gat_own", [P, T, 4 + HE])
        statistics(nc, core, core.x, "gat_stat")
        with nc.sbuf_tensor("gat_kept", [P, gat.tiles, 4 + HE], F32) as kept:
            project(nc, core, "gat_proj", core.x, HE, [(0, w["W_gat"])],
                    stores=[(table, "out", 0, HE, 4), (table, a_src, 0, 4, 0)],
                    to_sbuf=[(own_rows[:, :, 4:], 0)],
                    att=[(a_src, 0, 4, 4), (ma[:, :, 4:], 0, 4, 4)],
                    att_loads=[(0, w["att_src"].rearrange("(o h) e -> o (h e)", o=1)),
                               (1, w["att_dst"].rearrange("(o h) e -> o (h e)", o=1))])
            copy_all(nc, "gat_copy", [(ma[:, :, 0:4], a_src[:]), (own_rows[:, :, 0:4], a_src[:])])
            edge_max(nc, core, gat, "gat_max", 4, table, 4 + HE, kept[:, :, 0:4], ma[:, :, 0:4], kept=kept)
            gat_self(nc, core, acc, ma, own_rows)
            edge_sum(nc, core, gat, "gat_sum", acc, HE, kept=kept, heads=4, val=kept[:, :, 0:4], ma=ma, slope=0.2)
        gat_scores(nc, core, acc, scores, w)
        with nc.sbuf_tensor("gat_z", [P, T, D], F32) as z:
            normalize(nc, core, z, "gat_norm", add=False)
            mixture(nc, core, "m1", scores, "top", 2, z, w["W1"], w["b1"], w["W2"], w["b2"], ACT.Gelu)


def copy_all(nc, name, pairs):
    with Phase(nc, name) as ph:
        with nc.Block() as block:
            @block.vector
            def _(dve):
                for dst, src in pairs:
                    dve.tensor_copy(dst, src)


def layer2_gnn(nc, core, main, w):
    feats = nc.dram_tensor("l2_feats", [T * P, D], F32).ap()
    scores_d = nc.dram_tensor("l2_scores", [T * P, 4], F32).ap()
    own_part = nc.dram_tensor("l2_own", [T * P, 2 * D], F32).ap()
    with ExitStack() as ctx:
        sb = lambda n, s, dt=F32: ctx.enter_context(nc.sbuf_tensor(n, s, dt))
        wt = sb("l2_w", [P, DC, 2 * D])
        z_src = sb("l2_zsrc", [P, T, 4])
        ma = sb("l2_ma", [P, T, 2])
        score = sb("l2_score", [P, main.tiles, 1])
        load_transposed(nc, core, [(wt[:, :, 0:D], w["W_self"]), (wt[:, :, D:], w["W_func"])], "l2_turn")
        statistics(nc, core, core.x, "l2_stat")
        fill(nc, "l2_fill", [(z_src[:], 0.0), (ma[:], -FAR)])
        project(nc, core, "l2_proj", core.x, 2 * D, [], w_sb=wt, add_to_x=True,
                stores=[(feats, "out", D, 2 * D, 0), (own_part, "z", 0, D, 0), (own_part, "out", 0, D, D),
                        (scores_d, z_src, 0, 4, 0)],
                att=[(z_src[:, :, 0:1], D, 1, D), (ma[:, :, 1:2], D, 1, D)],
                att_loads=[(0, w["W_att"][0:1, 0:D]), (1, w["W_att"][0:1, D:2 * D])])
        edge_max(nc, core, main, "l2_max", 1, scores_d, 4, score, ma[:, :, 0:1], extra=main.extra)
        acc = sb("l2_acc", [P, T, D + 1])
        fill(nc, "l2_fill_acc", [(acc[:], 0.0)])
        edge_sum(nc, core, main, "l2_sum", acc, D, table=feats, heads=1, val=score, ma=ma, slope=0.01)
        finish_gnn(nc, core, "l2_finish", acc, 1, table=own_part, select=True)


def layer3_gnn(nc, core, src_d, dst_d, w):
    H, C = 4, D // 4
    table = nc.dram_tensor("l3_table", [T * P, D + 4], F32).ap()
    left = nc.dram_tensor("l3_left", [T * P, 4], F32).ap()
    with ExitStack() as ctx:
        sb = lambda n, s, dt=F32: ctx.enter_context(nc.sbuf_tensor(n, s, dt))
        al = sb("l3_al", [P, T, H])
        ar = sb("l3_ar", [P, T, H])
        statistics(nc, core, core.x, "l3_stat")
        project(nc, core, "l3_proj", core.x, D, [(0, w["weight"])],
                stores=[(table, "out", 0, D, 0), (left, al, 0, H, 0), (table, ar, 0, H, D)],
                att=[(al, 0, H, C), (ar, 0, H, C)],
                att_loads=[(0, w["attn_l"].rearrange("(o h) e -> o (h e)", o=1)),
                           (1, w["attn_r"].rearrange("(o h) e -> o (h e)", o=1))])
        with Phase(nc, "l3_mix") as ph:
            idx = ph.sb("idx", [P, T, 2], I32)
            ix = ph.sb("ix", [P, G4, 2], I32)
            rows = ph.sb("rows", [P, G4, D + 4])
            lrow = ph.sb("lrow", [P, G4, H])
            alpha = ph.sb("alpha", [P, T, H])
            ssum = ph.sb("ssum", [P, T])
            xt = ph.sb("xt", [P, T, D])
            prod = ph.sb("prod", [P, D])
            mixed = ph.sb("mixed", [P, 2, C])
            zeroed, listed, staged, taken, kept, own, ready, done, mix = [ph.sem(n) for n in (
                "zeroed", "listed", "staged", "taken", "kept", "own", "ready", "done", "mix")]
            got = [ph.gathered_sem(k) for k in range(G4)]
            with nc.Block() as block:
                @block.sync
                def _(sp):
                    sp.wait_ge(zeroed, 1)
                    with nc.allow_non_contiguous_dma("one number to a descriptor, 12500 of them"):
                        for k, v in enumerate((dst_d, src_d)):
                            sp.dma_start(idx[:, 0:T - 1, k], v[0:(T - 1) * P].rearrange("(t p) -> p t", p=P)
                                         ).then_inc(listed, 16)
                            sp.dma_start(idx[0:LAST, T - 1, k:k + 1], v[(T - 1) * P:N].rearrange("(p o) -> p o", o=1)
                                         ).then_inc(listed, 16)

                @block.scalar
                def _(act):
                    act.wait_ge(listed, 64)

                    def stage(t, slot):
                        wait_free(act, got[slot], (t - slot) * 8, t)
                        act.copy(ix[:, slot, :], idx[:, ds(t, 1), :].rearrange("p o k -> p (o k)")
                                 ).then_inc(staged, 1)
                    steps(act, T, [(0, stage)], unroll=G4)
                    act.wait_ge(ready, 1)
                    act.activation(alpha[:].rearrange("p t h -> p (t h)"), alpha[:].rearrange("p t h -> p (t h)"),
                                   ACT.Exp).then_inc(done, 1)

                @block.gpsimd
                def _(pool):
                    bound = pool.to_reg(N - 1)

                    def gather(t, slot):
                        wait_free(pool, kept, t - 3, t)
                        pool.wait_ge(staged, t + 1)
                        pool.sem_inc(taken, 1)
                        pool.indirect_dma_start(rows[:, slot, :], None, table,
                                                bass.IndirectOffsetOnAxis(ap=ix[:, slot, 0:1], axis=0),
                                                bounds_check=bound, oob_is_err=False).then_inc(got[slot], 16)
                        pool.indirect_dma_start(lrow[:, slot, :], None, left,
                                                bass.IndirectOffsetOnAxis(ap=ix[:, slot, 1:2], axis=0),
                                                bounds_check=bound, oob_is_err=False).then_inc(got[slot], 16)
                    steps(pool, T, [(0, gather)], unroll=G4)

                @block.vector
                def _(dve):
                    dve.memset(idx[:], 0).then_inc(zeroed, 1)

                    def keep(t, slot):
                        dve.wait_ge(got[slot], (t - slot) * 8 + 32)
                        copy_f(dve, xt[:, ds(t, 1), :], rows[:, slot, 0:D].unsqueeze(1))
                        dve.tensor_tensor(alpha[:, ds(t, 1), :], lrow[:, slot, :].unsqueeze(1),
                                          rows[:, slot, D:D + H].unsqueeze(1), ALU.add).then_inc(kept, 1)
                    steps(dve, T, [(0, keep)], unroll=G4)
                    dve.wait_ge(kept, T)
                    o = Own(dve, own, 16).at(0)
                    over = bc(ssum[:], 2, [P, T, H])
                    o.then(dve.scalar_tensor_tensor(out=alpha[:], in0=alpha[:], scalar=0.01, in1=alpha[:],
                                                    op0=ALU.mult, op1=ALU.max))
                    o.then(dve.tensor_reduce(ssum[:], alpha[:], AX.X, ALU.max))
                    dve.tensor_tensor(alpha[:], alpha[:], over, ALU.subtract).then_inc(ready, 1)
                    dve.wait_ge(done, 1)
                    o.then(dve.tensor_reduce(ssum[:], alpha[:], AX.X, ALU.add))
                    o.then(dve.reciprocal(ssum[:], ssum[:]))
                    o.then(dve.tensor_tensor(alpha[:], alpha[:], over, ALU.mult))
                    m = Own(dve, mix, 3)

                    def mixture_of_heads(t, par):
                        m.at(t)
                        wait_free(dve, mix, t * 3, t)
                        x = core.x[:, ds(t, 1), :].rearrange("p o (h c) -> p (o h) c", h=H)
                        m.then(dve.tensor_tensor(
                            prod[:].rearrange("p (h c) -> p h c", h=H),
                            xt[:, ds(t, 1), :].rearrange("p o (h c) -> p (o h) c", h=H),
                            bc(alpha[:, ds(t, 1), :].rearrange("p o h -> p (o h)"), 2, [P, H, C]), ALU.mult))
                        m.then(dve.tensor_reduce(mixed[:, par, :], prod[:].rearrange("p (h c) -> p c h", h=H),
                                                 AX.X, ALU.add))
                        m.mark(dve.tensor_tensor(x, x, bc(mixed[:, par, :], 1, [P, H, C]), ALU.add))
                    steps(dve, T, [(0, mixture_of_heads)])


LAYERS = ("L0_gnn_", "L0_ffn_", "L1_gnn_", "L1_ffn_", "L2_gnn_", "L2_ffn_", "L3_gnn_", "L3_ffn_")


def gnn_stack_kernel(nc, a, out):
    w = [{k[len(p):]: v for k, v in a.items() if k.startswith(p)} for p in LAYERS]
    E = a["src"].shape[0]
    ei = a["L1_ffn_edge_index"]
    with ExitStack() as ctx:
        core = Core(nc, ctx)
        make_constants(nc, core)
        load_x(nc, core, a["x"])
        with ExitStack() as c2:
            main = EdgeList(nc, c2, "main", E, 46)
            sort_edges(nc, core, main, a["src"], a["dst"], a["edge_attr_64"], w[4]["W_att"])
            layer0_gnn(nc, core, main, w[0])
            layer0_ffn(nc, core, w[1])
            with ExitStack() as c3:
                back = EdgeList(nc, c3, "back", E, 46)
                sort_edges(nc, core, back, a["dst"], a["src"])
                layer1_gnn(nc, core, back, w[2])
            with ExitStack() as c3:
                gat = EdgeList(nc, c3, "gat", ei.shape[1], 64)
                sort_edges(nc, core, gat, ei[0], ei[1])
                layer1_ffn(nc, core, gat, w[3])
            layer2_gnn(nc, core, main, w[4])
        layer2_ffn(nc, core, w[5])
        layer3_gnn(nc, core, a["src"], a["dst"], w[6])
        layer3_ffn(nc, core, w[7])
        store_x(nc, core, out)


def kernel(**inputs):
    import numpy as _np
    import concourse.bacc as _bacc
    from concourse import mybir as _mybir
    from concourse.bass_utils import run_bass_kernel_spmd as _run

    nc = _bacc.Bacc("TRN2", target_bir_lowering=False, num_devices=1)
    arrays, args = {}, {}
    for name in inputs:
        if name == "node_vec1":
            continue
        v = _np.ascontiguousarray(inputs[name])
        arrays[f"in_{name}"] = v
        args[name] = nc.dram_tensor(f"in_{name}", v.shape, _mybir.dt.from_np(v.dtype), kind="ExternalInput").ap()
    out = nc.dram_tensor("out_x", (N, D), _mybir.dt.float32, kind="ExternalOutput").ap()
    gnn_stack_kernel(nc, args, out)
    r = _run(nc, [arrays], core_ids=[0])
    return r.results[0]["out_x"]
```
